# Optimizing a Trainium2 kernel written in Bass

```python
import numpy as np
import jax
import jax.numpy as jnp

def _softmax(x, axis=-1):
    return jax.nn.softmax(x, axis=axis)

def _gelu(x):
    return jax.nn.gelu(x, approximate=True)

def _silu(x):
    return jax.nn.silu(x)

def _sigmoid(x):
    return jax.nn.sigmoid(x)

def _layernorm(x, axis=-1, eps=1e-05):
    m = jnp.mean(x, axis=axis, keepdims=True)
    v = jnp.var(x, axis=axis, keepdims=True)
    return (x - m) / jnp.sqrt(v + eps)

def _scatter_add(tgt, idx, src, axis=0):
    return tgt.at[idx].add(src)

def _segment_sum(src, seg, n):
    return jax.ops.segment_sum(src, seg, n)
kernel_name = 'mk_macaron_d1_jaxref_r2_b5610b'

def setup_inputs(seed: int=0):
    np.random.seed(seed)
    _w = jnp.asarray

    def _L0_attn_setup():
        import jax, jax.numpy as jnp
        import numpy as np
        N_HIDDEN = 512
        N_HEADS = 16
        HEAD_DIM = N_HIDDEN // N_HEADS
        KERNEL = 4
        GN_EPS = 1e-05

        def _short_conv_1d(x, weight):
            F, K = weight.shape
            xp = jnp.pad(x, ((0, 0), (K - 1, 0), (0, 0)))
            shifts = jnp.stack([xp[:, i:i + x.shape[1], :] for i in range(K)], axis=-1)
            return jnp.sum(shifts * weight[None, None, :, :], axis=-1)
        key = jax.random.key(seed)
        ks = jax.random.split(key, 16)
        B, S = (4, 2048)
        H, Hd = (N_HEADS, N_HIDDEN)
        sc = 0.02
        inp = {'x': jax.random.normal(ks[0], (B, S, Hd), dtype=jnp.float32), 'Wq': jax.random.normal(ks[1], (Hd, Hd), dtype=jnp.float32) * sc, 'bq': jnp.zeros((Hd,), jnp.float32), 'Wk': jax.random.normal(ks[2], (Hd, Hd), dtype=jnp.float32) * sc, 'bk': jnp.zeros((Hd,), jnp.float32), 'Wv': jax.random.normal(ks[3], (Hd, Hd), dtype=jnp.float32) * sc, 'bv': jnp.zeros((Hd,), jnp.float32), 'q_conv': jax.random.normal(ks[4], (Hd, KERNEL), dtype=jnp.float32) * sc, 'k_conv': jax.random.normal(ks[5], (Hd, KERNEL), dtype=jnp.float32) * sc, 'v_conv': jax.random.normal(ks[6], (Hd, KERNEL), dtype=jnp.float32) * sc, 'Wa': jax.random.normal(ks[7], (Hd, H), dtype=jnp.float32) * sc, 'ba': jnp.zeros((H,), jnp.float32), 'Wb': jax.random.normal(ks[8], (Hd, H), dtype=jnp.float32) * sc, 'bb': jnp.zeros((H,), jnp.float32), 'Wg': jax.random.normal(ks[9], (Hd, Hd), dtype=jnp.float32) * sc, 'bg': jnp.zeros((Hd,), jnp.float32), 'gn_scale': jnp.ones((Hd,), jnp.float32), 'gn_bias': jnp.zeros((Hd,), jnp.float32), 'Wo': jax.random.normal(ks[10], (Hd, Hd), dtype=jnp.float32) * sc, 'bo': jnp.zeros((Hd,), jnp.float32)}
        return inp
    _L0_attn_in = _L0_attn_setup()

    def _L0_ffn_setup():
        import jax, jax.numpy as jnp
        import numpy as np
        DIM = 512

        def _reference_tuple_inner(x, W_r, W_k, W_v, mu_r, mu_k):
            B, T, C = x.shape
            x_prev = jnp.concatenate([jnp.zeros((B, 1, C), x.dtype), x[:, :-1, :]], axis=1)
            xr = mu_r * x + (1.0 - mu_r) * x_prev
            xk = mu_k * x + (1.0 - mu_k) * x_prev
            r = jax.nn.sigmoid(jnp.einsum('btc,dc->btd', xr, W_r))
            k = jnp.einsum('btc,dc->btd', xk, W_k)
            k_act = jnp.square(jax.nn.relu(k))
            out = r * jnp.einsum('btc,dc->btd', k_act, W_v)
            new_state = x[:, -1, :]
            return (out, new_state)
        key = jax.random.key(seed)
        ks = jax.random.split(key, 6)
        B, T, C = (8, 1024, DIM)
        x = jax.random.normal(ks[0], (B, T, C), dtype=jnp.float32)
        s = 1.0 / np.sqrt(C)
        W_r = jax.random.uniform(ks[1], (C, C), jnp.float32, -s, s)
        W_k = jax.random.uniform(ks[2], (C, C), jnp.float32, -s, s)
        W_v = jax.random.uniform(ks[3], (C, C), jnp.float32, -s, s)
        mu_r = jax.random.uniform(ks[4], (C,), jnp.float32)
        mu_k = jax.random.uniform(ks[5], (C,), jnp.float32)
        return {'x': x, 'W_r': W_r, 'W_k': W_k, 'W_v': W_v, 'mu_r': mu_r, 'mu_k': mu_k}
    _L0_ffn_in = _L0_ffn_setup()
    _d = {'L0_attn_x': _L0_attn_in['x'], 'L0_attn_Wq': _L0_attn_in['Wq'], 'L0_attn_bq': _L0_attn_in['bq'], 'L0_attn_Wk': _L0_attn_in['Wk'], 'L0_attn_bk': _L0_attn_in['bk'], 'L0_attn_Wv': _L0_attn_in['Wv'], 'L0_attn_bv': _L0_attn_in['bv'], 'L0_attn_q_conv': _L0_attn_in['q_conv'], 'L0_attn_k_conv': _L0_attn_in['k_conv'], 'L0_attn_v_conv': _L0_attn_in['v_conv'], 'L0_attn_Wa': _L0_attn_in['Wa'], 'L0_attn_ba': _L0_attn_in['ba'], 'L0_attn_Wb': _L0_attn_in['Wb'], 'L0_attn_bb': _L0_attn_in['bb'], 'L0_attn_Wg': _L0_attn_in['Wg'], 'L0_attn_bg': _L0_attn_in['bg'], 'L0_attn_gn_scale': _L0_attn_in['gn_scale'], 'L0_attn_gn_bias': _L0_attn_in['gn_bias'], 'L0_attn_Wo': _L0_attn_in['Wo'], 'L0_attn_bo': _L0_attn_in['bo'], 'L0_ffn_W_r': _L0_ffn_in['W_r'], 'L0_ffn_W_k': _L0_ffn_in['W_k'], 'L0_ffn_W_v': _L0_ffn_in['W_v'], 'L0_ffn_mu_r': _L0_ffn_in['mu_r'], 'L0_ffn_mu_k': _L0_ffn_in['mu_k']}
    _x0 = _d['L0_attn_x']
    _d['L0_attn_x'] = jax.random.normal(jax.random.fold_in(jax.random.key(seed), 1), (8, 1024, 512), dtype=_x0.dtype)
    del _x0
    return _d

def reference(L0_attn_x, L0_attn_Wq, L0_attn_bq, L0_attn_Wk, L0_attn_bk, L0_attn_Wv, L0_attn_bv, L0_attn_q_conv, L0_attn_k_conv, L0_attn_v_conv, L0_attn_Wa, L0_attn_ba, L0_attn_Wb, L0_attn_bb, L0_attn_Wg, L0_attn_bg, L0_attn_gn_scale, L0_attn_gn_bias, L0_attn_Wo, L0_attn_bo, L0_ffn_W_r, L0_ffn_W_k, L0_ffn_W_v, L0_ffn_mu_r, L0_ffn_mu_k):

    def _L0_attn_ref(x, Wq, bq, Wk, bk, Wv, bv, q_conv, k_conv, v_conv, Wa, ba, Wb, bb, Wg, bg, gn_scale, gn_bias, Wo, bo):
        import jax, jax.numpy as jnp
        import numpy as np
        N_HIDDEN = 512
        N_HEADS = 16
        HEAD_DIM = N_HIDDEN // N_HEADS
        KERNEL = 4
        GN_EPS = 1e-05

        def _short_conv_1d(x, weight):
            F, K = weight.shape
            xp = jnp.pad(x, ((0, 0), (K - 1, 0), (0, 0)))
            shifts = jnp.stack([xp[:, i:i + x.shape[1], :] for i in range(K)], axis=-1)
            return jnp.sum(shifts * weight[None, None, :, :], axis=-1)
        B, S, _ = x.shape
        h, d = (N_HEADS, HEAD_DIM)
        q = jax.nn.silu(_short_conv_1d(x @ Wq + bq, q_conv)).reshape(B, S, h, d)
        q = q / (jnp.linalg.norm(q, axis=-1, keepdims=True) + 1e-06)
        k = jax.nn.silu(_short_conv_1d(x @ Wk + bk, k_conv)).reshape(B, S, h, d)
        k = k / (jnp.linalg.norm(k, axis=-1, keepdims=True) + 1e-06)
        v = jax.nn.silu(_short_conv_1d(x @ Wv + bv, v_conv)).reshape(B, S, h, d)
        alpha = jax.nn.sigmoid(x @ Wa + ba)
        beta = jax.nn.sigmoid(x @ Wb + bb)
        out_gate = jax.nn.silu(x @ Wg + bg)
        qT = jnp.transpose(q, (1, 0, 2, 3))
        kT = jnp.transpose(k, (1, 0, 2, 3))
        vT = jnp.transpose(v, (1, 0, 2, 3))
        aT = jnp.transpose(alpha, (1, 0, 2))
        bT = jnp.transpose(beta, (1, 0, 2))

        def _step(Sst, inputs):
            q_t, k_t, v_t, a_t, b_t = inputs
            a = a_t[:, :, None, None]
            b = b_t[:, :, None, None]
            Sk = jnp.einsum('bhde,bhe->bhd', Sst, k_t)
            delta_gated = v_t - a_t[:, :, None] * Sk
            update = b * jnp.einsum('bhd,bhe->bhde', delta_gated, k_t)
            Sst = a * Sst + update
            o_t = jnp.einsum('bhde,bhe->bhd', Sst, q_t)
            return (Sst, o_t)
        S0 = jnp.zeros((B, h, d, d), dtype=x.dtype)
        _, outs = jax.lax.scan(_step, S0, (qT, kT, vT, aT, bT))
        outs = jnp.transpose(outs, (1, 0, 2, 3)).reshape(B, S, N_HIDDEN)
        g = outs.reshape(B, S, h, d)
        mu = jnp.mean(g, axis=(1, 3), keepdims=True)
        var = jnp.mean(jnp.square(g), axis=(1, 3), keepdims=True) - jnp.square(mu)
        g = (g - mu) * jax.lax.rsqrt(var + GN_EPS)
        y = g.reshape(B, S, N_HIDDEN) * gn_scale + gn_bias
        return out_gate * y @ Wo + bo

    def _L0_ffn_ref(x, W_r, W_k, W_v, mu_r, mu_k):
        import jax, jax.numpy as jnp
        import numpy as np
        DIM = 512

        def _reference_tuple_inner(x, W_r, W_k, W_v, mu_r, mu_k):
            B, T, C = x.shape
            x_prev = jnp.concatenate([jnp.zeros((B, 1, C), x.dtype), x[:, :-1, :]], axis=1)
            xr = mu_r * x + (1.0 - mu_r) * x_prev
            xk = mu_k * x + (1.0 - mu_k) * x_prev
            r = jax.nn.sigmoid(jnp.einsum('btc,dc->btd', xr, W_r))
            k = jnp.einsum('btc,dc->btd', xk, W_k)
            k_act = jnp.square(jax.nn.relu(k))
            out = r * jnp.einsum('btc,dc->btd', k_act, W_v)
            new_state = x[:, -1, :]
            return (out, new_state)
        return _reference_tuple_inner(x, W_r, W_k, W_v, mu_r, mu_k)[0]
    x = L0_attn_x
    x = x + 0.5 * _L0_ffn_ref(_layernorm(x, axis=-1), L0_ffn_W_r, L0_ffn_W_k, L0_ffn_W_v, L0_ffn_mu_r, L0_ffn_mu_k)
    x = x + _L0_attn_ref(_layernorm(x, axis=-1), L0_attn_Wq, L0_attn_bq, L0_attn_Wk, L0_attn_bk, L0_attn_Wv, L0_attn_bv, L0_attn_q_conv, L0_attn_k_conv, L0_attn_v_conv, L0_attn_Wa, L0_attn_ba, L0_attn_Wb, L0_attn_bb, L0_attn_Wg, L0_attn_bg, L0_attn_gn_scale, L0_attn_gn_bias, L0_attn_Wo, L0_attn_bo)
    x = x + 0.5 * _L0_ffn_ref(_layernorm(x, axis=-1), L0_ffn_W_r, L0_ffn_W_k, L0_ffn_W_v, L0_ffn_mu_r, L0_ffn_mu_k)
    return x

_drawn_inputs = setup_inputs


def setup_inputs(seed=0):
    import zlib

    import numpy as np

    out = dict(_drawn_inputs(seed))
    spreads = {'L0_attn_bq': (0.0, 0.8),
     'L0_attn_bk': (0.0, 0.8),
     'L0_attn_bv': (0.0, 0.8),
     'L0_attn_ba': (0.0, 2.0),
     'L0_attn_bb': (0.0, 0.8),
     'L0_attn_bg': (0.0, 0.8),
     'L0_attn_gn_scale': (1.0, 0.6),
     'L0_attn_gn_bias': (0.0, 0.742),
     'L0_attn_bo': (0.0, 0.1)}
    factors = {'L0_attn_Wa': 8.0, 'L0_attn_Wb': 8.0, 'L0_ffn_W_r': 3.182, 'L0_ffn_mu_r': 6.516}
    for name, (base, spread) in spreads.items():
        noise = np.random.default_rng([zlib.crc32(name.encode()), seed]).standard_normal(out[name].shape)
        drawn = base * np.exp(spread * noise) if base else spread * noise
        out[name] = jnp.asarray(drawn.astype(out[name].dtype))
    for name, factor in factors.items():
        out[name] = (out[name] * factor).astype(out[name].dtype)
    return out
```

```python
from contextlib import ExitStack

import concourse.bass as bass
from concourse import mybir

F32 = mybir.dt.float32
F32R = mybir.dt.float32r
ALU = mybir.AluOpType
ACT = mybir.ActivationFunctionType

P = 128
C = 512
KT = C // P
B, S = 8, 1024
TOK = 512
NT = B * S // TOK
TPB = S // TOK
H, HD = 16, 32
HG = P // HD
CH = 32
NCH = S // CH
CPT = TOK // CH
TAPS = 4
LN_EPS = 1e-5
NQ, NK_, NV, NA, NB = range(5)


def split_weight(nc, dve, staged, hi, lo, done):
    nc.vector.tensor_copy(hi, staged).then_inc(done[0], 1)
    done[1] += 1
    dve.wait_ge(done[0], done[1])
    nc.vector.tensor_tensor(lo, staged, hi.bitcast(F32), ALU.subtract).then_inc(done[0], 1)
    done[1] += 1


def product(nc, out, w_hi, w_lo, m, x_hi, x_lo, width=P):
    terms = [(w, x) for w, x in ((w_hi, x_hi), (w_hi, x_lo), (w_lo, x_hi))]
    last = None
    for k in range(KT):
        for n, (w, x) in enumerate(terms):
            last = nc.tensor.matmul(out, w[:, k, m * width:(m + 1) * width], x[:, k, :],
                                    start=(k == 0 and n == 0), stop=(k == KT - 1 and n == 2))
    return last


def build_identity(nc, pool, ident, done):
    nc.gpsimd.memset(ident, 0.0).then_inc(done, 1)
    pool.wait_ge(done, 1)
    nc.gpsimd.affine_select(out=ident, in_=ident, compare_op=ALU.not_equal, fill=1.0, base=0,
                            pattern=[[-1, P]], channel_multiplier=1).then_inc(done, 1)


def ffn_phase(nc, tag, src, dst, w_dram, mu_dram):
    with ExitStack() as ctx:
        def sb(name, shape, dt=F32):
            return ctx.enter_context(nc.sbuf_tensor(f"{tag}_{name}", shape, dt))

        def sem(name):
            return nc.alloc_semaphore(f"{tag}_{name}")

        W = {n: (sb(f"w{n}h", [P, KT, C], F32R), sb(f"w{n}l", [P, KT, C], F32R)) for n in "rkv"}
        mu = sb("mu", [P, 2, KT])
        mean_w = sb("mean_w", [P, P])
        start_mask = sb("start_mask", [P, NT, KT])
        x = sb("x", [P, KT, TOK])
        xc = sb("xc", [P, KT, TOK])
        xn = sb("xn", [P, KT, TOK + 1])
        diff = sb("diff", [P, KT, TOK])
        mix = {n: sb(f"mix{n}", [P, KT, TOK]) for n in "rk"}
        mix_h = {n: sb(f"mix{n}h", [P, KT, TOK], F32R) for n in "rk"}
        mix_l = {n: sb(f"mix{n}l", [P, KT, TOK], F32R) for n in "rk"}
        gate = sb("gate", [P, KT, TOK])
        act2 = sb("act2", [P, KT, TOK])
        act_h = sb("act_h", [P, KT, TOK], F32R)
        act_l = sb("act_l", [P, KT, TOK], F32R)
        xres = sb("xres", [P, KT, TOK])
        out = sb("out", [P, KT, TOK])
        half = sb("half", [P, 2, TOK])
        half2 = sb("half2", [P, 2, TOK])
        sum1 = sb("sum1", [P, TOK])
        sum2 = sb("sum2", [P, TOK])
        ident, ones = sb("ident", [P, P]), sb("ones", [P, P])
        var_tok, std_tok, rstd_tok = (sb(n, [P, KT]) for n in ("var_tok", "std_tok", "rstd_tok"))
        rstd_diag = sb("rstd_diag", [P, KT, P])
        ps_mean = ctx.enter_context(nc.psum_tensor(f"{tag}_mean", [P, TOK], F32))
        ps_rstd = ctx.enter_context(nc.psum_tensor(f"{tag}_rstd", [P, TOK], F32))
        ring = [ctx.enter_context(nc.psum_tensor(f"{tag}_ring{n}", [P, TOK], F32)) for n in range(6)]

        w_loaded, w_split, consts = sem("w_loaded"), sem("w_split"), sem("consts")
        x_loaded, xres_loaded, stored = sem("x_loaded"), sem("xres_loaded"), sem("stored")
        halved, summed, mean_done, centred = sem("halved"), sem("summed"), sem("mean_done"), sem("centred")
        squared, halved2, summed2, var_done = sem("squared"), sem("halved2"), sem("summed2"), sem("var_done")
        ident_step, inverted, diagonal, spread = sem("ident_step"), sem("inverted"), sem("diagonal"), sem("spread")
        dve_step = sem("dve_step")
        mixed, mix_high, mix_low = sem("mixed"), sem("mix_high"), sem("mix_low")
        r_done, k_done, v_done = sem("r_done"), sem("k_done"), sem("v_done")
        gated, relued, act_sq, act_high, act_low = sem("gated"), sem("relued"), sem("act_sq"), sem("act_high"), sem("act_low")
        var_copied, std_ready = sem("var_copied"), sem("std_ready")
        v_used, out_ready = sem("v_used"), sem("out_ready")

        block = ctx.enter_context(nc.Block())

        @block.sync
        def _(sp):
            for n, stage in zip("rkv", (mix["r"], mix["k"], act2)):
                sp.dma_start(stage[:], w_dram[n]).then_inc(w_loaded, 16)
            sp.dma_start(mu[:], mu_dram).then_inc(w_loaded, 16)
            sp.dma_start(x[:], src[0, :, :, :]).then_inc(x_loaded, 16)

            def load_x(t):
                sp.wait_ge(centred, t)
                sp.dma_start(x[:], src[t, :, :, :]).then_inc(x_loaded, 16)

            def slot(t, ahead):
                sp.wait_ge(out_ready, t)
                sp.dma_start(xres[:], src[t, :, :, :]).then_inc(xres_loaded, 16)
                if ahead:
                    load_x(t + 2)
                sp.wait_ge(out_ready, t + 1)
                sp.dma_start(dst[t, :, :, :], out[:]).then_inc(stored, 16)

            load_x(1)
            with sp.Fori(0, NT - 2) as t:
                slot(t, True)
            slot(NT - 2, False)
            slot(NT - 1, False)
            sp.wait_ge(stored, 16 * NT)

        @block.vector
        def _(dve):
            PER = 2

            nc.vector.memset(mean_w[:], 1.0 / C)
            nc.vector.memset(ones[:], 1.0)
            nc.vector.memset(start_mask[:], 1.0).then_inc(dve_step, 1)
            nc.vector.memset(xn[:, :, TOK:TOK + 1], 0.0)
            dve.wait_ge(dve_step, 1)
            nc.vector.memset(start_mask[:, 0:NT:TPB, :], 0.0).then_inc(dve_step, 1)
            dve.wait_ge(dve_step, 2)
            dve.wait_ge(w_loaded, 16 * 4)
            count = [w_split, 0]
            for n, stage in zip("rkv", (mix["r"], mix["k"], act2)):
                split_weight(nc, dve, stage[:], W[n][0][:], W[n][1][:], count)
            dve.wait_ge(w_split, count[1])
            nc.vector.memset(var_tok[:], 0.0).then_inc(consts, 1)

            def sums(t):
                dve.wait_ge(x_loaded, 16 * t + 16)
                nc.vector.tensor_tensor(half[:], x[:, 0:2, :], x[:, 2:4, :], ALU.add).then_inc(halved, 1)
                dve.wait_ge(halved, t + 1)
                nc.vector.tensor_tensor(sum1[:], half[:, 0, :], half[:, 1, :], ALU.add).then_inc(summed, 1)

            def centre(t):
                dve.wait_ge(mean_done, t + 1)
                nc.vector.tensor_tensor(xc[:], x[:], ps_mean[:].unsqueeze(1).to_broadcast([P, KT, TOK]),
                                        ALU.subtract).then_inc(centred, 1)

            def mixes(t, n, nth):
                for k in range(KT):
                    last = nc.vector.scalar_tensor_tensor(
                        out=mix[n][:, k, :], in0=diff[:, k, :], scalar=mu[:, nth, k:k + 1],
                        in1=xn[:, k, 0:TOK], op0=ALU.mult, op1=ALU.add)
                last.then_inc(mixed, 1)

            def mix_rest(t, n, nth):
                dve.wait_ge(mix_high, 2 * t + nth + 1)
                nc.vector.tensor_tensor(mix_l[n][:], mix[n][:], mix_h[n][:].bitcast(F32), ALU.subtract).then_inc(mix_low, 1)

            def deviations(t):
                dve.wait_ge(var_done, t + 1)
                nc.vector.tensor_scalar_add(var_tok[:], ps_mean[:, 0:KT], LN_EPS).then_inc(var_copied, 1)
                dve.wait_ge(std_ready, t + 1)
                nc.vector.reciprocal(rstd_tok[:], std_tok[:]).then_inc(inverted, 1)
                dve.wait_ge(inverted, t + 1)
                nc.vector.tensor_tensor(rstd_diag[:], ident[:].unsqueeze(1).to_broadcast([P, KT, P]),
                                        rstd_tok[:].unsqueeze(2).to_broadcast([P, KT, P]), ALU.mult).then_inc(diagonal, 1)

            def normalise(t):
                nc.vector.tensor_tensor(xn[:, :, 0:1], xn[:, :, TOK:TOK + 1],
                                        start_mask[:, bass.ds(t, 1), :].rearrange("p a k -> p k a"), ALU.mult).then_inc(dve_step, 1)
                dve.wait_ge(dve_step, PER * t + 3)
                dve.wait_ge(spread, t + 1)
                nc.vector.tensor_tensor(xn[:, :, 1:TOK + 1], xc[:], ps_rstd[:].unsqueeze(1).to_broadcast([P, KT, TOK]),
                                        ALU.mult).then_inc(dve_step, 1)

            def differ(t):
                dve.wait_ge(dve_step, PER * t + 4)
                nc.vector.tensor_tensor(diff[:], xn[:, :, 1:TOK + 1], xn[:, :, 0:TOK], ALU.subtract).then_inc(consts, 1)
                dve.wait_ge(consts, t + 2)

            def act_rest(t, m):
                dve.wait_ge(act_high, KT * t + m + 1)
                nc.vector.tensor_tensor(act_l[:, m, :], act2[:, m, :], act_h[:, m, :].bitcast(F32),
                                        ALU.subtract).then_inc(act_low, 1)

            def slot(t, ahead):
                if ahead:
                    centre(t + 1)
                    deviations(t + 1)
                    normalise(t + 1)
                    differ(t + 1)
                act_rest(t, 0)
                if ahead:
                    mixes(t + 1, "r", 0)
                for m in range(1, KT):
                    act_rest(t, m)
                if ahead:
                    mix_rest(t + 1, "r", 0)
                    mixes(t + 1, "k", 1)
                    mix_rest(t + 1, "k", 1)
                if ahead == 2:
                    sums(t + 2)
                for m in range(KT):
                    dve.wait_ge(v_done, KT * t + m + 1)
                    dve.wait_ge(gated, KT * t + m + 1)
                    nc.vector.scalar_tensor_tensor(out=gate[:, m, :], in0=ring[(8 + m) % 6][:], scalar=0.5,
                                                   in1=gate[:, m, :], op0=ALU.mult, op1=ALU.mult).then_inc(v_used, 1)

            dve.wait_ge(ident_step, 2)
            sums(0)
            centre(0)
            deviations(0)
            normalise(0)
            differ(0)
            for nth, n in enumerate("rk"):
                mixes(0, n, nth)
                mix_rest(0, n, nth)
            sums(1)
            with dve.Fori(0, NT - 2) as t:
                slot(t, 2)
            slot(NT - 2, 1)
            slot(NT - 1, 0)

        @block.gpsimd
        def _(pool):
            def squares(t):
                pool.wait_ge(squared, t + 1)
                nc.gpsimd.tensor_tensor(half2[:], diff[:, 0:2, :], diff[:, 2:4, :], ALU.add).then_inc(halved2, 1)
                pool.wait_ge(halved2, t + 1)
                nc.gpsimd.tensor_tensor(sum2[:], half2[:, 0, :], half2[:, 1, :], ALU.add).then_inc(summed2, 1)

            def slot(t, more):
                if more:
                    squares(t + 1)
                pool.wait_ge(xres_loaded, 16 * t + 16)
                pool.wait_ge(stored, 16 * t)
                for m in range(KT):
                    pool.wait_ge(v_used, KT * t + m + 1)
                    last = nc.gpsimd.tensor_tensor(out[:, m, :], gate[:, m, :], xres[:, m, :], ALU.add)
                last.then_inc(out_ready, 1)

            build_identity(nc, pool, ident[:], ident_step)
            squares(0)
            with pool.Fori(0, NT - 1) as t:
                slot(t, True)
            slot(NT - 1, False)

        @block.scalar
        def _(act):
            def square(t):
                act.wait_ge(centred, t + 1)
                nc.scalar.activation(diff[:], xc[:], ACT.Square).then_inc(squared, 1)

            def deviation(t):
                act.wait_ge(var_copied, t + 1)
                nc.scalar.activation(std_tok[:], var_tok[:], ACT.Sqrt).then_inc(std_ready, 1)

            def high(t, n, nth):
                act.wait_ge(mixed, 2 * t + nth + 1)
                act.wait_ge((r_done, k_done)[nth], KT * t)
                nc.scalar.activation(mix_h[n][:], mix[n][:], ACT.Copy).then_inc(mix_high, 1)

            def gates(t, m):
                act.wait_ge(r_done, KT * t + m + 1)
                if m == 0:
                    act.wait_ge(out_ready, t)
                nc.scalar.activation(gate[:, m, :], ring[m][:], ACT.Sigmoid).then_inc(gated, 1)

            def activated(t, m):
                act.wait_ge(k_done, KT * t + m + 1)
                act.wait_ge(act_low, KT * t)
                nc.scalar.activation(act2[:, m, :], ring[(4 + m) % 6][:], ACT.Relu).then_inc(relued, 1)
                act.wait_ge(relued, KT * t + m + 1)
                nc.scalar.activation(act2[:, m, :], act2[:, m, :], ACT.Square).then_inc(act_sq, 1)
                act.wait_ge(act_sq, KT * t + m + 1)
                act.wait_ge(v_done, KT * t)
                nc.scalar.activation(act_h[:, m, :], act2[:, m, :], ACT.Copy).then_inc(act_high, 1)

            def slot(t, more):
                if more:
                    square(t + 1)
                for m in range(3):
                    gates(t, m)
                gates(t, 3)
                if more:
                    deviation(t + 1)
                activated(t, 0)
                activated(t, 1)
                activated(t, 2)
                activated(t, 3)
                if more:
                    high(t + 1, "r", 0)
                if more:
                    high(t + 1, "k", 1)

            act.wait_ge(consts, 1)
            square(0)
            deviation(0)
            high(0, "r", 0)
            high(0, "k", 1)
            with act.Fori(0, NT - 1) as t:
                slot(t, True)
            slot(NT - 1, False)

        @block.tensor
        def _(pe):
            def mean(t):
                pe.wait_ge(summed, t + 1)
                nc.tensor.matmul(ps_mean[:], mean_w[:], sum1[:], start=True, stop=True).then_inc(mean_done, 1)

            def var(t):
                pe.wait_ge(summed2, t + 1)
                for j in range(KT):
                    last = nc.tensor.matmul(ps_mean[:, j:j + 1], sum2[:, j * P:(j + 1) * P], mean_w[:, 0:1], start=(j == 0),
                                            stop=True, skip_group_check=True)
                last.then_inc(var_done, 1)

            def spread_rstd(t):
                pe.wait_ge(diagonal, t + 1)
                nc.tensor.matmul(ps_rstd[:], ones[:], rstd_diag[:].rearrange("p j n -> p (j n)"), start=True,
                                 stop=True).then_inc(spread, 1)

            def project(t, n, nth, m, done):
                if m == 0:
                    pe.wait_ge(mix_low, 2 * t + nth + 1)
                if nth == 0:
                    if m == 0:
                        pe.wait_ge(relued, KT * t)
                    if m == 2:
                        pe.wait_ge(v_used, KT * t)
                elif m == 2:
                    pe.wait_ge(gated, KT * t + 2)
                product(nc, ring[(4 * nth + m) % 6][:], *W[n], m, mix_h[n], mix_l[n]).then_inc(done, 1)

            def slot(t, more):
                if more:
                    mean(t + 1)
                for m in range(KT):
                    project(t, "r", 0, m, r_done)
                if more:
                    var(t + 1)
                project(t, "k", 1, 0, k_done)
                if more:
                    spread_rstd(t + 1)
                project(t, "k", 1, 1, k_done)
                for m in range(2, KT):
                    project(t, "k", 1, m, k_done)
                pe.wait_ge(act_low, KT * t + KT)
                pe.wait_ge(gated, KT * t + KT)
                pe.wait_ge(relued, KT * t + KT)
                for m in range(KT):
                    product(nc, ring[(8 + m) % 6][:], *W["v"], m, act_h, act_l).then_inc(v_done, 1)

            pe.wait_ge(consts, 1)
            pe.wait_ge(ident_step, 2)
            mean(0)
            var(0)
            spread_rstd(0)
            with pe.Fori(0, NT - 1) as t:
                slot(t, True)
            slot(NT - 1, False)


def attn_in_phase(nc, tag, src, streams, gate_dram, w_dram, wab_dram, bias_dram, ab_bias_dram, conv_dram):
    with ExitStack() as ctx:
        def sb(name, shape, dt=F32):
            return ctx.enter_context(nc.sbuf_tensor(f"{tag}_{name}", shape, dt))

        def pb(name):
            return ctx.enter_context(nc.psum_tensor(f"{tag}_ps_{name}", [P, TOK], F32))

        def sem(name):
            return nc.alloc_semaphore(f"{tag}_{name}")

        W = {n: (sb(f"w{n}h", [P, KT, C], F32R), sb(f"w{n}l", [P, KT, C], F32R)) for n in "qkvg"}
        wab_h, wab_l = sb("wab_h", [P, KT, P], F32R), sb("wab_l", [P, KT, P], F32R)
        bias = sb("bias", [P, 4, KT])
        ab_bias = sb("ab_bias", [P, 1])
        taps = sb("taps", [P, 3, KT, TAPS])
        mean_w = sb("mean_w", [P, P])
        start_mask = sb("start_mask", [P, NT, 3 * KT, TAPS - 1])
        head_sum = sb("head_sum", [P, 2 * KT, P])
        spread_f = sb("spread_f", [P, P])
        spread = sb("spread", [P, 4 * KT, P], F32R)
        x = sb("x", [P, KT, TOK])
        xc = sb("xc", [P, KT, TOK])
        xh, xl = sb("xh", [P, KT, TOK], F32R), sb("xl", [P, KT, TOK], F32R)
        sq = sb("sq", [P, 4, TOK])
        half, half2 = sb("half", [P, 2, TOK]), sb("half2", [P, 2, TOK])
        sum1, sum2 = sb("sum1", [P, TOK]), sb("sum2", [P, TOK])
        ident, ones = sb("ident", [P, P]), sb("ones", [P, P])
        var_tok, std_tok, rstd_tok = (sb(n, [P, KT]) for n in ("var_tok", "std_tok", "rstd_tok"))
        rstd_diag = sb("rstd_diag", [P, KT, P])
        padded = [sb(f"padded{r}", [P, TOK + TAPS - 1]) for r in range(3)]
        tail = sb("tail", [P, 3 * KT, TAPS - 1])
        bias_tap = sb("bias_tap", [P, 3 * KT])
        term = sb("term", [P, TOK])
        conv = [sb(f"conv{r}", [P, TOK]) for r in range(3)]
        rows = sb("rows", [P, TOK])
        rows_h, rows_l = sb("rows_h", [P, TOK], F32R), sb("rows_l", [P, TOK], F32R)
        buf = sb("buf", [P, CPT, 5, KT, CH])
        gate = sb("gate", [P, KT, TOK])
        flat = buf[:].rearrange("p c s g i -> p (c s g i)")
        stage = [flat[:, n * KT * C:(n + 1) * KT * C].rearrange("p (k n) -> p k n", k=KT) for n in range(4)]
        ps_mean, ps_rstd, ps_rows = pb("mean"), pb("rstd"), pb("rows")
        ring = [pb(f"ring{n}") for n in range(4)]

        w_loaded, w_split, padded_w = sem("w_loaded"), sem("w_split"), sem("padded_w")
        consts_pool, sel_step, ready = sem("consts_pool"), sem("sel_step"), sem("ready")
        x_loaded, stored, gate_stored = sem("x_loaded"), sem("stored"), sem("gate_stored")
        halved, summed, mean_done, centred = sem("halved"), sem("summed"), sem("mean_done"), sem("centred")
        squared, halved2, summed2, var_done = sem("squared"), sem("halved2"), sem("summed2"), sem("var_done")
        ident_step, inverted, diagonal, spread_done = sem("ident_step"), sem("inverted"), sem("diagonal"), sem("spread_done")
        var_copied, std_ready, norm_step = sem("var_copied"), sem("std_ready"), sem("norm_step")
        x_high, x_low = sem("x_high"), sem("x_low")
        group_done, ab_done, sigmoided = sem("group_done"), sem("ab_done"), sem("sigmoided")
        biased, conv_step, silued = sem("biased"), sem("conv_step"), sem("silued")
        pool_conv, tails_masked, pool_turns = sem("pool_conv"), sem("tails_masked"), sem("pool_turns")
        q_squared, heads_summed, rooted = sem("q_squared"), sem("heads_summed"), sem("rooted")
        rows_step = sem("rows_step")
        ring_act, ring_dve, gate_ready = sem("ring_act"), sem("ring_dve"), sem("gate_ready")

        D_STEPS, D_UNITS, P_STEPS, P_UNITS = TAPS + 1, 8, 2 * TAPS, 4

        def dve_unit(u):
            return u // 3 * 2 + u % 3

        def wait_convolved(eng, t, u):
            if u % 3 == 2:
                eng.wait_ge(pool_conv, P_STEPS * (P_UNITS * t + u // 3 + 1))
            else:
                eng.wait_ge(conv_step, D_STEPS * (D_UNITS * t + dve_unit(u) + 1))

        block = ctx.enter_context(nc.Block())

        @block.sync
        def _(sp):
            for n, s in zip("qkvg", stage):
                sp.dma_start(s, w_dram[n]).then_inc(w_loaded, 16)
            for dst, s in ((bias[:], bias_dram), (taps[:], conv_dram)):
                sp.dma_start(dst, s).then_inc(w_loaded, 16)
            sp.wait_ge(padded_w, 2)
            sp.dma_start(xc[:, :, 0:2 * H], wab_dram).then_inc(w_loaded, 16)
            sp.dma_start(ab_bias[0:2 * H, :], ab_bias_dram).then_inc(w_loaded, 16)
            sp.dma_start(x[:], src[0, :, :, :]).then_inc(x_loaded, 16)

            def load_x(t):
                sp.wait_ge(centred, t)
                sp.dma_start(x[:], src[t, :, :, :]).then_inc(x_loaded, 16)

            def slot(t, ahead):
                if ahead:
                    load_x(t + 2)
                sp.wait_ge(gate_ready, KT * t + KT)
                sp.dma_start(gate_dram[t, :, :, :], gate[:]).then_inc(gate_stored, 16)
                sp.wait_ge(ring_act, 8 * t + 8)
                sp.wait_ge(ring_dve, 8 * t + 8)
                sp.dma_start(streams[bass.ds(t * CPT, CPT), :, :].rearrange("c p f -> p c f"),
                             buf[:].rearrange("p c s g i -> p c (s g i)")).then_inc(stored, 16)

            load_x(1)
            with sp.Fori(0, NT - 2) as t:
                slot(t, True)
            slot(NT - 2, False)
            slot(NT - 1, False)
            sp.wait_ge(stored, 16 * NT)
            sp.wait_ge(gate_stored, 16 * NT)

        @block.vector
        def _(dve):
            ROWS = 4
            nc.vector.memset(xc[:], 0.0).then_inc(padded_w, 1)
            nc.vector.memset(ab_bias[:], 0.0).then_inc(padded_w, 1)
            nc.vector.memset(mean_w[:], 1.0 / C)
            nc.vector.memset(ones[:], 1.0)
            nc.vector.memset(tail[:], 0.0)
            nc.vector.memset(rows[:], 0.0)
            nc.vector.memset(start_mask[:], 1.0).then_inc(w_split, 1)
            dve.wait_ge(w_split, 1)
            nc.vector.memset(start_mask[:, 0:NT:TPB, :, :], 0.0)
            dve.wait_ge(w_loaded, 16 * 8)
            nc.vector.tensor_tensor(bias_tap[:].rearrange("p (j k) -> p j k", k=KT), bias[:, 0:3, :], taps[:, :, :, TAPS - 1],
                                    ALU.mult)
            count = [w_split, 1]
            for n, s in zip("qkvg", stage):
                split_weight(nc, dve, s, W[n][0][:], W[n][1][:], count)
            split_weight(nc, dve, xc[:, :, 0:P], wab_h[:], wab_l[:], count)
            dve.wait_ge(w_split, count[1])
            nc.vector.tensor_copy(rows_h[:], rows[:])
            nc.vector.tensor_copy(rows_l[:], rows[:]).then_inc(ready, 1)

            def sums(t):
                dve.wait_ge(x_loaded, 16 * t + 16)
                nc.vector.tensor_tensor(half[:], x[:, 0:2, :], x[:, 2:4, :], ALU.add).then_inc(halved, 1)
                dve.wait_ge(halved, t + 1)
                nc.vector.tensor_tensor(sum1[:], half[:, 0, :], half[:, 1, :], ALU.add).then_inc(summed, 1)

            def centre(t):
                dve.wait_ge(mean_done, t + 1)
                nc.vector.tensor_tensor(xc[:], x[:], ps_mean[:].unsqueeze(1).to_broadcast([P, KT, TOK]),
                                        ALU.subtract).then_inc(centred, 1)

            def deviations(t):
                dve.wait_ge(var_done, t + 1)
                nc.vector.tensor_scalar_add(var_tok[:], ps_mean[:, 0:KT], LN_EPS).then_inc(var_copied, 1)
                dve.wait_ge(std_ready, t + 1)
                nc.vector.reciprocal(rstd_tok[:], std_tok[:]).then_inc(inverted, 1)
                dve.wait_ge(inverted, t + 1)
                nc.vector.tensor_tensor(rstd_diag[:], ident[:].unsqueeze(1).to_broadcast([P, KT, P]),
                                        rstd_tok[:].unsqueeze(2).to_broadcast([P, KT, P]), ALU.mult).then_inc(diagonal, 1)

            def normalise(t):
                dve.wait_ge(spread_done, t + 1)
                nc.vector.tensor_tensor(xc[:], xc[:], ps_rstd[:].unsqueeze(1).to_broadcast([P, KT, TOK]),
                                        ALU.mult).then_inc(norm_step, 1)

            def low(t):
                dve.wait_ge(x_high, t + 1)
                nc.vector.tensor_tensor(xl[:], xc[:], xh[:].bitcast(F32), ALU.subtract).then_inc(x_low, 1)

            def mask_tails(t):
                dve.wait_ge(conv_step, D_STEPS * D_UNITS * t)
                dve.wait_ge(pool_conv, P_STEPS * P_UNITS * t)
                nc.vector.tensor_tensor(tail[:].unsqueeze(1), tail[:].unsqueeze(1), start_mask[:, bass.ds(t, 1), :, :],
                                        ALU.mult).then_inc(tails_masked, 1)
                dve.wait_ge(tails_masked, t + 1)

            def convolve(t, u):
                pad, out = padded[u % 3], conv[u % 3]
                at = D_STEPS * (D_UNITS * t + dve_unit(u))
                dve.wait_ge(biased, 12 * t + u + 1)
                nc.vector.tensor_copy(pad[:, 0:TAPS - 1], tail[:, u, :]).then_inc(conv_step, 1)
                dve.wait_ge(conv_step, at + 1)
                nc.vector.tensor_copy(tail[:, u, :], pad[:, TOK:TOK + TAPS - 1]).then_inc(conv_step, 1)
                for n in range(TAPS - 1):
                    dve.wait_ge(conv_step, at + 2 + n)
                    nc.vector.scalar_tensor_tensor(out=out[:], in0=pad[:, n:n + TOK], scalar=taps[:, u // KT, u % KT, n:n + 1],
                                                   in1=out[:], op0=ALU.mult, op1=ALU.add).then_inc(conv_step, 1)

            def norms(t):
                dve.wait_ge(rooted, t + 1)
                nc.vector.tensor_scalar_add(rows[2 * H:4 * H, :], rows[2 * H:4 * H, :], 1e-6).then_inc(rows_step, 1)
                dve.wait_ge(rows_step, ROWS * t + 1)
                nc.vector.reciprocal(rows[2 * H:4 * H, :], rows[2 * H:4 * H, :]).then_inc(rows_step, 1)
                dve.wait_ge(rows_step, ROWS * t + 2)
                dve.wait_ge(sigmoided, t + 1)
                nc.vector.tensor_copy(rows_h[0:4 * H, :], rows[0:4 * H, :]).then_inc(rows_step, 1)
                dve.wait_ge(rows_step, ROWS * t + 3)
                nc.vector.tensor_tensor(rows_l[0:4 * H, :], rows[0:4 * H, :], rows_h[0:4 * H, :].bitcast(F32),
                                        ALU.subtract).then_inc(rows_step, 1)

            def slot(t, ahead):
                mask_tails(t)
                if ahead:
                    centre(t + 1)
                for u in range(12):
                    if u % 3 < 2:
                        convolve(t, u)
                if ahead:
                    deviations(t + 1)
                norms(t)
                if ahead:
                    normalise(t + 1)
                for n in range(2 * KT):
                    if ahead and n == KT:
                        low(t + 1)
                    dve.wait_ge(group_done, 32 * t + 16 + 2 * n + 2)
                    j, g = divmod(n, KT)
                    view = buf[:, :, j, g, :]
                    nc.vector.tensor_tensor(view, view, ring[(2 * n + 1) % 4][:].rearrange("p (c i) -> p c i", i=CH),
                                            ALU.mult).then_inc(ring_dve, 1)
                if ahead == 2:
                    sums(t + 2)

            dve.wait_ge(ident_step, 2)
            sums(0)
            centre(0)
            deviations(0)
            normalise(0)
            low(0)
            sums(1)
            with dve.Fori(0, NT - 2) as t:
                slot(t, 2)
            slot(NT - 2, 1)
            slot(NT - 1, 0)

        @block.gpsimd
        def _(pool):
            build_identity(nc, pool, ident[:], ident_step)
            nc.gpsimd.memset(head_sum[:], 1.0).then_inc(sel_step, 1)
            pool.wait_ge(sel_step, 1)
            pattern = [[HG * HD, 2 * KT], [-HD, P]]
            base = 2 * H * HD
            nc.gpsimd.affine_select(out=head_sum[:], in_=head_sum[:], compare_op=ALU.is_ge, fill=0.0, base=base,
                                    pattern=pattern, channel_multiplier=1).then_inc(sel_step, 1)
            pool.wait_ge(sel_step, 2)
            nc.gpsimd.affine_select(out=head_sum[:], in_=head_sum[:], compare_op=ALU.is_ge, fill=0.0, base=HD - 1 - base,
                                    pattern=[[-s, n] for s, n in pattern], channel_multiplier=-1).then_inc(sel_step, 1)
            for n in range(4 * KT):
                nc.gpsimd.memset(spread_f[:], 0.0).then_inc(sel_step, 1)
                pool.wait_ge(sel_step, 3 * n + 4)
                view = spread_f[:].rearrange("p (h d) -> p h d", h=HG)
                nc.gpsimd.affine_select(out=view, in_=view, compare_op=ALU.not_equal, fill=1.0, base=-HG * n,
                                        pattern=[[-1, HG], [0, HD]], channel_multiplier=1).then_inc(sel_step, 1)
                pool.wait_ge(sel_step, 3 * n + 5)
                last = nc.gpsimd.tensor_copy(spread[:, n, :], spread_f[:])
                last.then_inc(sel_step, 1)
                pool.wait_ge(sel_step, 3 * n + 6)
            nc.gpsimd.memset(half2[:, 0, 0:1], 0.0).then_inc(consts_pool, 1)

            def squares(t):
                pool.wait_ge(squared, t + 1)
                nc.gpsimd.tensor_tensor(half2[:], gate[:, 0:2, :], gate[:, 2:4, :], ALU.add).then_inc(halved2, 1)
                pool.wait_ge(halved2, t + 1)
                nc.gpsimd.tensor_tensor(sum2[:], half2[:, 0, :], half2[:, 1, :], ALU.add).then_inc(summed2, 1)

            def convolve(t, u):
                at = P_STEPS * (P_UNITS * t + u // 3)
                pad, out = padded[2], conv[2]

                def turn():
                    pool.sem_inc(pool_turns, 1)

                pool.wait_ge(biased, 12 * t + u + 1)
                turn()
                nc.gpsimd.tensor_copy(pad[:, 0:TAPS - 1], tail[:, u, :]).then_inc(pool_conv, 1)
                pool.wait_ge(pool_conv, at + 1)
                turn()
                nc.gpsimd.tensor_copy(tail[:, u, :], pad[:, TOK:TOK + TAPS - 1]).then_inc(pool_conv, 1)
                for n in range(TAPS - 1):
                    pool.wait_ge(pool_conv, at + 2 + 2 * n)
                    turn()
                    nc.gpsimd.tensor_scalar(term[:], pad[:, n:n + TOK], taps[:, u // KT, u % KT, n:n + 1], 1.0,
                                            ALU.mult, ALU.mult).then_inc(pool_conv, 1)
                    pool.wait_ge(pool_conv, at + 3 + 2 * n)
                    nc.gpsimd.tensor_tensor(out[:], out[:], term[:], ALU.add).then_inc(pool_conv, 1)

            def slot(t, more):
                pool.wait_ge(tails_masked, t + 1)
                convolve(t, 2)
                if more:
                    squares(t + 1)
                for u in (5, 8, 11):
                    convolve(t, u)

            squares(0)
            with pool.Fori(0, NT - 1) as t:
                slot(t, True)
            slot(NT - 1, False)

        @block.scalar
        def _(act):
            def square(t):
                act.wait_ge(centred, t + 1)
                nc.scalar.activation(gate[:], xc[:], ACT.Square).then_inc(squared, 1)

            def deviation(t):
                act.wait_ge(var_copied, t + 1)
                nc.scalar.activation(std_tok[:], var_tok[:], ACT.Sqrt).then_inc(std_ready, 1)

            def high(t):
                act.wait_ge(norm_step, t + 1)
                nc.scalar.activation(xh[:], xc[:], ACT.Copy).then_inc(x_high, 1)

            def shift(t, u):
                act.wait_ge(group_done, 32 * t + u + 1)
                if u >= 3:
                    wait_convolved(act, t, u - 3)
                nc.scalar.activation(padded[u % 3][:, TAPS - 1:], ring[u % 4][:], ACT.Identity,
                                     bias=bias[:, u // KT, u % KT:u % KT + 1])
                if u < 3:
                    act.wait_ge(silued, 12 * t)
                else:
                    act.wait_ge(silued, 12 * t + u - 2)
                nc.scalar.activation(conv[u % 3][:], ring[u % 4][:], ACT.Identity, bias=bias_tap[:, u:u + 1],
                                     scale=taps[:, u // KT, u % KT, TAPS - 1:TAPS]).then_inc(biased, 1)

            def silu(t, u):
                j, m = divmod(u, KT)
                wait_convolved(act, t, u)
                if u == 0:
                    act.wait_ge(stored, 16 * t)
                view = buf[:, :, j, m, :]
                nc.scalar.activation(view, conv[u % 3][:].rearrange("p (c i) -> p c i", i=CH), ACT.Silu).then_inc(silued, 1)
                if j < 2:
                    act.wait_ge(silued, 12 * t + u + 1)
                    if u < 4:
                        act.wait_ge(heads_summed, 8 * t)
                    else:
                        act.wait_ge(heads_summed, 8 * t + u - 3)
                    nc.scalar.activation(sq[:, u % 4, :].rearrange("p (c i) -> p c i", i=CH), view,
                                         ACT.Square).then_inc(q_squared, 1)

            def rows_copy(t, n):
                act.wait_ge(group_done, 32 * t + 16 + 2 * n + 1)
                nc.scalar.activation(buf[:, :, NA + n // KT, n % KT, :],
                                     ring[2 * n % 4][:].rearrange("p (c i) -> p c i", i=CH), ACT.Copy).then_inc(ring_act, 1)

            def slot(t, more):
                act.wait_ge(ab_done, t + 1)
                act.wait_ge(rows_step, 4 * t)
                nc.scalar.activation(rows[0:2 * H, :], ps_rows[0:2 * H, :], ACT.Sigmoid,
                                     bias=ab_bias[0:2 * H, :]).then_inc(sigmoided, 1)
                if more:
                    act.wait_ge(gate_stored, 16 * t)
                    square(t + 1)
                for u in range(12):
                    shift(t, u)
                    if u > 1:
                        silu(t, u - 2)
                if more:
                    deviation(t + 1)
                act.wait_ge(heads_summed, 8 * t + 8)
                nc.scalar.activation(rows[2 * H:4 * H, :], ps_rows[2 * H:4 * H, :], ACT.Sqrt).then_inc(rooted, 1)
                if more:
                    act.wait_ge(halved2, t + 2)
                act.wait_ge(gate_stored, 16 * t)
                silu(t, 10)
                for m in range(KT):
                    if m == 2:
                        silu(t, 11)
                    act.wait_ge(group_done, 32 * t + 12 + m + 1)
                    nc.scalar.activation(gate[:, m, :], ring[m][:], ACT.Silu, bias=bias[:, 3, m:m + 1]).then_inc(gate_ready, 1)
                for n in range(KT):
                    rows_copy(t, n)
                if more:
                    high(t + 1)
                for n in range(KT, 2 * KT):
                    rows_copy(t, n)

            act.wait_ge(ready, 1)
            act.wait_ge(consts_pool, 1)
            square(0)
            deviation(0)
            high(0)
            with act.Fori(0, NT - 1) as t:
                slot(t, True)
            slot(NT - 1, False)

        @block.tensor
        def _(pe):
            def mean(t):
                pe.wait_ge(summed, t + 1)
                nc.tensor.matmul(ps_mean[:], mean_w[:], sum1[:], start=True, stop=True).then_inc(mean_done, 1)

            def var(t):
                pe.wait_ge(summed2, t + 1)
                for j in range(KT):
                    last = nc.tensor.matmul(ps_mean[:, j:j + 1], sum2[:, j * P:(j + 1) * P], mean_w[:, 0:1], start=(j == 0),
                                            stop=True, skip_group_check=True)
                last.then_inc(var_done, 1)

            def spread_rstd(t):
                pe.wait_ge(diagonal, t + 1)
                nc.tensor.matmul(ps_rstd[:], ones[:], rstd_diag[:].rearrange("p j n -> p (j n)"), start=True,
                                 stop=True).then_inc(spread_done, 1)

            def head_sums(t, n):
                pe.wait_ge(q_squared, 8 * t + n + 1)
                if n == 0:
                    pe.wait_ge(sigmoided, t + 1)
                nc.tensor.matmul(ps_rows[:], head_sum[:, n, :], sq[:, n % 4, :], start=(n == 0),
                                 stop=(n == 7)).then_inc(heads_summed, 1)

            def slot(t, more):
                if more:
                    mean(t + 1)
                pe.wait_ge(x_low, t + 1)
                pe.wait_ge(rooted, t)
                product(nc, ps_rows[:], wab_h, wab_l, 0, xh, xl).then_inc(ab_done, 1)
                for u in range(16):
                    j, m = divmod(u, KT)
                    if u < 4:
                        if u == 0:
                            pe.wait_ge(ring_dve, 8 * t)
                            pe.wait_ge(ring_act, 8 * t)
                    else:
                        pe.wait_ge(biased, 12 * t + u - 3)
                    product(nc, ring[u % 4][:], *W["qkvg"[j]], m, xh, xl).then_inc(group_done, 1)
                    if 4 <= u < 12:
                        head_sums(t, u - 4)
                    if more and u == 11:
                        var(t + 1)
                    if more and u == 14:
                        spread_rstd(t + 1)
                for n in range(16):
                    if n < 4:
                        pe.wait_ge(gate_ready, 4 * t + n + 1)
                    else:
                        pe.wait_ge((ring_act, ring_dve)[n % 2], 8 * t + n // 2 - 1)
                    if n == 0:
                        pe.wait_ge(rows_step, 4 * t + 4)
                    which = spread[:, n // 2 + n % 2 * 2 * KT, :]
                    nc.tensor.matmul(ring[n % 4][:], which, rows_h[:], start=True, stop=False)
                    nc.tensor.matmul(ring[n % 4][:], which, rows_l[:], start=False, stop=True).then_inc(group_done, 1)

            pe.wait_ge(ready, 1)
            pe.wait_ge(consts_pool, 1)
            pe.wait_ge(ident_step, 2)
            mean(0)
            var(0)
            spread_rstd(0)
            with pe.Fori(0, NT - 1) as t:
                slot(t, True)
            slot(NT - 1, False)


DELTA, NOT_FIRST, FIRST, IN_BLOCK, OFF_BLOCK = range(5)
BLOCK = 8


def recurrence_masks():
    import numpy as np
    j, i = np.arange(P)[:, None] % CH, np.arange(CH)[None, :]
    kinds = [i == j, (i > 0) & (j >= 0), (i == 0) & (j >= 0),
             (i > j) & (i // BLOCK == j // BLOCK), (i > j) & (i // BLOCK != j // BLOCK)]
    return np.stack([np.tile(k, (1, KT)) for k in kinds], axis=1).astype(np.float32)


def recurrence_phase(nc, tag, streams, masks_dram, o_all):
    with ExitStack() as ctx:
        def sb(name, shape, dt=F32):
            return ctx.enter_context(nc.sbuf_tensor(f"{tag}_{name}", shape, dt))

        def pb(name, width):
            t = ctx.enter_context(nc.psum_tensor(f"{tag}_ps_{name}", [P, KT * 128], F32))
            return t[:].rearrange("p (g x) -> p g x", g=KT)[:, :, 0:width * CH].rearrange("p g (w i) -> p g w i", i=CH)

        def sem(name):
            return nc.alloc_semaphore(f"{tag}_{name}")

        tile = [P, KT, CH]
        pair = [P, KT, 2, CH]
        masks = sb("masks", [P, 5, KT * CH])
        inb = [sb(f"inb{s}", [P, 5, KT, CH]) for s in range(2)]
        vt = [sb(f"vt{s}", tile) for s in range(2)]
        kb = [sb(f"kb{s}", tile) for s in range(2)]
        decay0, decay_first = sb("decay0", tile), sb("decay_first", tile)
        dmat, gam = sb("dmat", tile), sb("gam", tile)
        d_in, d_off = sb("d_in", tile), sb("d_off", tile)
        kb_t = sb("kb_t", tile)
        gkq = [sb(f"gkq{s}", pair) for s in range(2)]
        pk = [sb(f"pk{s}", pair) for s in range(2)]
        g_last = [sb(f"g_last{s}", [P, KT, 1]) for s in range(2)]
        a_in, a_in_t, a_off = sb("a_in", tile), sb("a_in_t", tile), sb("a_off", tile)
        r2, r5 = sb("r2", pair), sb("r5", pair)
        b2_t, b4_t, t2 = sb("b2_t", tile), sb("b4_t", tile), sb("t2", tile)
        t8_t, f_t, f2_t, y = sb("t8_t", tile), sb("f_t", tile), sb("f2_t", tile), sb("y", tile)
        inv_t = [sb(f"inv_t{s}", tile) for s in range(2)]
        state = sb("state", [P, B, KT, CH])
        s_cur, s_cur_t, s_decayed = sb("s_cur", tile), sb("s_cur_t", tile), sb("s_decayed", tile)
        z_t, z, u = sb("z_t", tile), sb("z", tile), sb("u", tile)
        bank = [pb(f"inv{n}", 2) for n in range(4)]
        ps_chain, ps_u = pb("chain", 3), pb("u", 1)

        masks_loaded, state_zero, pe_turns = sem("masks_loaded"), sem("state_zero"), sem("pe_turns")
        in_loaded, v_loaded = [sem("in0"), sem("in1")], [sem("v0"), sem("v1")]
        kb_ready, decays_ready, dmat_ready, gam_ready = sem("kb"), sem("decays"), sem("dmat"), sem("gam")
        masked, kbt_ready, gkq_ready, kw_ready, glast_ready = sem("masked"), sem("kbt"), sem("gkq"), sem("kw"), sem("glast")
        gp_done, ain_ready, aint_ready, aoff_ready, pt_ready, t1_ready = (
            sem("gp_done"), sem("ain"), sem("aint"), sem("aoff"), sem("pt"), sem("t1"))
        s1_done, b2_ready, b2t_ready = sem("s1_done"), sem("b2"), sem("b2t")
        s2_done, b4t_ready, t2_ready = sem("s2_done"), sem("b4t"), sem("t2r")
        s3_done, t8_ready, t8t_ready = sem("s3_done"), sem("t8"), sem("t8t")
        s4_done, f_ready, ft_ready = sem("s4_done"), sem("f"), sem("ft")
        s5_done, f2t_ready, y_ready = sem("s5_done"), sem("f2t"), sem("yr")
        s6_done, inv_ready = sem("s6_done"), sem("inv")
        cur_ready, curt_ready, sdec_ready = sem("cur"), sem("curt"), sem("sdec")
        c1_done, zt_ready, z_ready = sem("c1_done"), sem("zt"), sem("zr")
        c2_done, u_ready, c3_done, o_ready, state_ready = sem("c2_done"), sem("ur"), sem("c3_done"), sem("o"), sem("state_new")

        def mask(kind):
            return masks[:, kind, :].rearrange("p (g i) -> p g i", g=KT)

        block = ctx.enter_context(nc.Block())

        @block.sync
        def _(sp):
            def load_in(s, b, c):
                sp.dma_start(inb[s][:].rearrange("p s g i -> p (s g i)"),
                             streams[bass.ds(b * NCH + c, 1), :, :].rearrange("c p f -> p (c f)")).then_inc(in_loaded[s], 16)

            def load_v(s, b, c):
                sp.dma_start(vt[s][:].rearrange("p g i -> p (g i)"),
                             streams[bass.ds(b * NCH + c, 1), :, NV * KT * CH:(NV + 1) * KT * CH].rearrange("c p f -> p (c f)")
                             ).then_inc(v_loaded[s], 16)

            sp.dma_start(masks[:], masks_dram).then_inc(masks_loaded, 16)
            for s in range(2):
                load_in(s, s, 0)
                load_v(s, s, 0)

            def refill(n, s, b, c):
                sp.wait_ge(gp_done, n + 1)
                sp.wait_ge(gkq_ready, n + 1)
                load_in(s, b, c)
                sp.wait_ge(zt_ready, n + 1)
                load_v(s, b, c)

            with sp.Fori(1, B // 2) as q:
                for s in range(2):
                    refill(q * 2 + s - 2, s, q * 2 + s, 0)
            with sp.Fori(1, NCH) as c:
                with sp.Fori(0, B // 2) as q:
                    for s in range(2):
                        refill(c * B + q * 2 + s - 2, s, q * 2 + s, c)
            for s in range(2):
                refill(NCH * B - 2 + s, s, s, 0)
            for s in range(2):
                sp.wait_ge(in_loaded[s], 16 * (NCH * B // 2 + 1))
                sp.wait_ge(v_loaded[s], 16 * (NCH * B // 2 + 1))

        @block.gpsimd
        def _(pool):
            mul = ALU.mult

            def scale_inputs(m, s, it):
                pool.wait_ge(in_loaded[s], it * 16 + 16)
                pool.wait_ge(gp_done, m)
                pool.wait_ge(kbt_ready, m)
                nc.gpsimd.tensor_tensor(kb[s][:], inb[s][:, NK_], inb[s][:, NB], mul).then_inc(kb_ready, 1)
                pool.wait_ge(gam_ready, m)
                pool.wait_ge(dmat_ready, m)
                nc.gpsimd.tensor_tensor(decay0[:], inb[s][:, NA], mask(NOT_FIRST), mul)
                nc.gpsimd.tensor_tensor(decay_first[:], inb[s][:, NA], mask(FIRST), mul).then_inc(decays_ready, 1)
                pool.wait_ge(dmat_ready, m + 1)
                pool.wait_ge(aoff_ready, m)
                pool.wait_ge(ain_ready, m)
                nc.gpsimd.tensor_tensor(d_in[:], dmat[:], mask(IN_BLOCK), mul)
                nc.gpsimd.tensor_tensor(d_off[:], dmat[:], mask(OFF_BLOCK), mul).then_inc(masked, 1)

            def scale_more(m, s, first):
                pool.wait_ge(gam_ready, m + 1)
                if not first:
                    pool.wait_ge(sdec_ready, m - 1)
                    pool.wait_ge(c1_done, m - 1)
                nc.gpsimd.tensor_tensor(gkq[s][:, :, 0, :], inb[s][:, NK_], gam[:], mul)
                nc.gpsimd.tensor_tensor(gkq[s][:, :, 1, :], inb[s][:, NQ], gam[:], mul)
                nc.gpsimd.tensor_copy(g_last[s][:], gam[:, :, CH - 1:CH]).then_inc(gkq_ready, 1)
                pool.wait_ge(kbt_ready, m + 1)
                if not first:
                    pool.wait_ge(c3_done, m - 1)
                nc.gpsimd.tensor_tensor(pk[s][:, :, 1, :], kb_t[:], dmat[:, :, CH - 1:CH].to_broadcast(tile),
                                        mul).then_inc(kw_ready, 1)

            def first_inverse(m):
                pool.wait_ge(ain_ready, m + 1)
                pool.wait_ge(t2_ready, m)
                nc.gpsimd.tensor_tensor(r2[:, :, 1, :], mask(DELTA), a_in[:], ALU.subtract).then_inc(t1_ready, 1)

            def decay_state(n, s):
                pool.wait_ge(cur_ready, n + 1)
                pool.wait_ge(state_ready, n)
                pool.wait_ge(gkq_ready, n + 1)
                nc.gpsimd.tensor_tensor(s_decayed[:], s_cur[:], g_last[s][:].to_broadcast(tile), mul).then_inc(sdec_ready, 1)

            pool.wait_ge(masks_loaded, 16)
            scale_inputs(0, 0, 0)
            scale_more(0, 0, True)
            first_inverse(0)
            scale_inputs(1, 1, 0)
            with pool.Fori(0, NCH) as c:
                with pool.Fori(0, B // 2) as q:
                    for s in range(2):
                        n = c * B + q * 2 + s
                        first_inverse(n + 1)
                        decay_state(n, s)
                        scale_more(n + 1, 1 - s, False)
                        scale_inputs(n + 2, s, c * (B // 2) + q + 1)

        @block.vector
        def _(dve):
            tr = nc.vector.transpose

            def scans(m, s):
                dve.wait_ge(decays_ready, m + 1)
                dve.wait_ge(kw_ready, m)
                dve.wait_ge(pt_ready, m)
                dve.wait_ge(masked, m)
                flat = "p g i -> p (g i)"
                nc.vector.tensor_tensor_scan(dmat[:].rearrange(flat), decay0[:].rearrange(flat), masks[:, DELTA, :], 0.0,
                                             ALU.mult, ALU.add).then_inc(dmat_ready, 1)
                dve.wait_ge(gkq_ready, m)
                nc.vector.tensor_tensor_scan(gam[:].rearrange(flat), decay0[:].rearrange(flat), decay_first[:].rearrange(flat),
                                             0.0, ALU.mult, ALU.add).then_inc(gam_ready, 1)
                dve.wait_ge(kb_ready, m + 1)
                tr(kb_t[:], kb[s][:]).then_inc(kbt_ready, 1)

            def triangles(m, s, first):
                dve.wait_ge(gp_done, m + 1)
                dve.wait_ge(masked, m + 1)
                dve.wait_ge(s1_done, m)
                dve.wait_ge(t1_ready, m)
                nc.vector.tensor_tensor(a_in[:], bank[0][:, :, 1, :], d_in[:], ALU.mult).then_inc(ain_ready, 1)
                dve.wait_ge(ain_ready, m + 1)
                tr(a_in_t[:], a_in[:]).then_inc(aint_ready, 1)
                dve.wait_ge(s4_done, m)
                nc.vector.tensor_tensor(a_off[:], bank[0][:, :, 1, :], d_off[:], ALU.mult).then_inc(aoff_ready, 1)
                if not first:
                    dve.wait_ge(c3_done, m - 1)
                nc.vector.tensor_tensor(pk[s][:, :, 0, :], bank[0][:, :, 0, :], dmat[:], ALU.mult).then_inc(pt_ready, 1)

            def residual(n, s, it):
                dve.wait_ge(v_loaded[s], it * 16 + 16)
                dve.wait_ge(c1_done, n + 1)
                dve.wait_ge(z_ready, n)
                nc.vector.tensor_tensor(z_t[:], vt[s][:], ps_chain[:, :, 0, :], ALU.subtract).then_inc(zt_ready, 1)
                dve.wait_ge(zt_ready, n + 1)
                dve.wait_ge(c2_done, n)
                tr(z[:], z_t[:]).then_inc(z_ready, 1)

            def squared(m):
                dve.wait_ge(b2_ready, m + 1)
                tr(b2_t[:], r2[:, :, 0, :]).then_inc(b2t_ready, 1)

            def fourth(m):
                dve.wait_ge(s2_done, m + 1)
                tr(b4_t[:], bank[2][:, :, 0, :]).then_inc(b4t_ready, 1)
                dve.wait_ge(t1_ready, m + 1)
                nc.vector.tensor_tensor(t2[:], r2[:, :, 1, :], bank[2][:, :, 1, :], ALU.add).then_inc(t2_ready, 1)

            def eighth(m):
                dve.wait_ge(s3_done, m + 1)
                dve.wait_ge(t2_ready, m + 1)
                nc.vector.tensor_tensor(r5[:, :, 1, :], t2[:], bank[3][:, :, 0, :], ALU.add).then_inc(t8_ready, 1)
                dve.wait_ge(t8_ready, m + 1)
                tr(t8_t[:], r5[:, :, 1, :]).then_inc(t8t_ready, 1)

            def between(m):
                dve.wait_ge(f_ready, m + 1)
                tr(f_t[:], r5[:, :, 0, :]).then_inc(ft_ready, 1)

            def between2(m):
                dve.wait_ge(s5_done, m + 1)
                tr(f2_t[:], bank[1][:, :, 0, :]).then_inc(f2t_ready, 1)
                nc.vector.tensor_tensor(y[:], r5[:, :, 1, :], bank[1][:, :, 1, :], ALU.subtract).then_inc(y_ready, 1)

            def inverse(m, s, first):
                dve.wait_ge(s6_done, m + 1)
                dve.wait_ge(y_ready, m + 1)
                if not first:
                    dve.wait_ge(c2_done, m - 1)
                nc.vector.tensor_tensor(inv_t[s][:], y[:], bank[2][:, :, 0, :], ALU.add).then_inc(inv_ready, 1)

            def new_state(n, b):
                dve.wait_ge(o_ready, n + 1)
                dve.wait_ge(sdec_ready, n + 1)
                nc.vector.tensor_tensor(state[:, bass.ds(b, 1), :, :].rearrange("p a g i -> p (a g) i"), s_decayed[:],
                                        ps_chain[:, :, 2, :], ALU.add).then_inc(state_ready, 1)

            def turn_state(n):
                dve.wait_ge(cur_ready, n + 1)
                dve.wait_ge(c1_done, n)
                tr(s_cur_t[:], s_cur[:]).then_inc(curt_ready, 1)

            nc.vector.memset(state[:], 0.0).then_inc(state_zero, 1)
            dve.wait_ge(masks_loaded, 16)
            scans(0, 0)
            triangles(0, 0, True)
            squared(0)
            fourth(0)
            eighth(0)
            between(0)
            between2(0)
            inverse(0, 0, True)
            scans(1, 1)
            turn_state(0)
            with dve.Fori(0, NCH) as c:
                with dve.Fori(0, B // 2) as q:
                    for s in range(2):
                        n = c * B + q * 2 + s
                        triangles(n + 1, 1 - s, False)
                        residual(n, s, c * (B // 2) + q)
                        squared(n + 1)
                        fourth(n + 1)
                        eighth(n + 1)
                        between(n + 1)
                        new_state(n, q * 2 + s)
                        between2(n + 1)
                        inverse(n + 1, 1 - s, False)
                        scans(n + 2, s)
                        turn_state(n + 1)

        @block.scalar
        def _(act):
            def power(m):
                act.wait_ge(s1_done, m + 1)
                act.wait_ge(s2_done, m)
                nc.scalar.activation(r2[:, :, 0, :], bank[1][:, :, 0, :], ACT.Copy).then_inc(b2_ready, 1)

            def coupling(m):
                act.wait_ge(s4_done, m + 1)
                act.wait_ge(s5_done, m)
                nc.scalar.activation(r5[:, :, 0, :], bank[0][:, :, 0, :], ACT.Copy).then_inc(f_ready, 1)

            def update(n):
                act.wait_ge(c2_done, n + 1)
                act.wait_ge(c3_done, n)
                nc.scalar.activation(u[:], ps_u[:, :, 0, :], ACT.Copy).then_inc(u_ready, 1)

            def output(n, b, c):
                act.wait_ge(c3_done, n + 1)
                nc.scalar.activation(o_all[:, bass.ds(b, 1), :, bass.ds(c * CH, CH)].rearrange("p a g i -> p (a g) i"),
                                     ps_chain[:, :, 1, :], ACT.Copy).then_inc(o_ready, 1)

            def current(n, b):
                act.wait_ge(sdec_ready, n)
                act.wait_ge(curt_ready, n)
                nc.scalar.activation(s_cur[:], state[:, bass.ds(b, 1), :, :].rearrange("p a g i -> p (a g) i"),
                                     ACT.Copy).then_inc(cur_ready, 1)

            act.wait_ge(state_zero, 1)
            power(0)
            coupling(0)
            current(0, 0)
            with act.Fori(0, NCH) as c:
                with act.Fori(0, B // 2) as q:
                    for s in range(2):
                        n = c * B + q * 2 + s
                        power(n + 1)
                        update(n)
                        coupling(n + 1)
                        output(n, q * 2 + s, c)
                        act.wait_ge(state_ready, n)
                        if s == 0:
                            current(n + 1, q * 2 + 1)
                        else:
                            current(n + 1, (q + 1) % (B // 2) * 2)

        @block.tensor
        def _(pe):
            def per_head(out, lhs_t, rhs, done, restart=True):
                pe.sem_inc(pe_turns, 1)
                for g in range(KT):
                    for h in range(HG):
                        rows = slice(h * HD, (h + 1) * HD)
                        last = nc.tensor.matmul(out(rows, g), lhs_t(rows, g), rhs(rows, g), start=restart and g == 0,
                                                stop=True, skip_group_check=True)
                last.then_inc(done, 1)

            def scores(m, s):
                pe.wait_ge(kb_ready, m + 1)
                pe.wait_ge(f_ready, m)
                per_head(lambda r, g: bank[0][r, g, :, :], lambda r, g: kb[s][r, g, :],
                         lambda r, g: inb[s][r, NQ:NK_ + 1, g, :], gp_done)

            def square(m):
                pe.wait_ge(aint_ready, m + 1)
                pe.wait_ge(y_ready, m)
                per_head(lambda r, g: bank[1][r, g, 0, :], lambda r, g: a_in_t[r, g, :], lambda r, g: a_in[r, g, :], s1_done)

            def fourth(m):
                pe.wait_ge(b2t_ready, m + 1)
                pe.wait_ge(t1_ready, m + 1)
                pe.wait_ge(inv_ready, m)
                per_head(lambda r, g: bank[2][r, g, :, :], lambda r, g: b2_t[r, g, :], lambda r, g: r2[r, g, :, :], s2_done)

            def eighth(m):
                pe.wait_ge(t2_ready, m + 1)
                pe.wait_ge(b4t_ready, m + 1)
                pe.wait_ge(t8_ready, m)
                per_head(lambda r, g: bank[3][r, g, 0, :], lambda r, g: b4_t[r, g, :], lambda r, g: t2[r, g, :], s3_done)

            def coupling(m):
                pe.wait_ge(t8t_ready, m + 1)
                pe.wait_ge(aoff_ready, m + 1)
                pe.wait_ge(pt_ready, m + 1)
                per_head(lambda r, g: bank[0][r, g, 0, :], lambda r, g: t8_t[r, g, :], lambda r, g: a_off[r, g, :], s4_done)

            def coupling2(m):
                pe.wait_ge(ft_ready, m + 1)
                per_head(lambda r, g: bank[1][r, g, :, :], lambda r, g: f_t[r, g, :], lambda r, g: r5[r, g, :, :], s5_done)

            def inverse(m):
                pe.wait_ge(f2t_ready, m + 1)
                pe.wait_ge(y_ready, m + 1)
                per_head(lambda r, g: bank[2][r, g, 0, :], lambda r, g: f2_t[r, g, :], lambda r, g: y[r, g, :], s6_done)

            def from_state(n, s):
                pe.wait_ge(curt_ready, n + 1)
                pe.wait_ge(gkq_ready, n + 1)
                pe.wait_ge(state_ready, n)
                per_head(lambda r, g: ps_chain[r, g, 0:2, :], lambda r, g: s_cur_t[r, g, :], lambda r, g: gkq[s][r, g, :, :], c1_done)

            def solve(n, s):
                pe.wait_ge(z_ready, n + 1)
                pe.wait_ge(inv_ready, n + 1)
                pe.wait_ge(u_ready, n)
                per_head(lambda r, g: ps_u[r, g, 0, :], lambda r, g: inv_t[s][r, g, :], lambda r, g: z[r, g, :], c2_done)

            def into_state(n, s):
                pe.wait_ge(u_ready, n + 1)
                pe.wait_ge(kw_ready, n + 1)
                per_head(lambda r, g: ps_chain[r, g, 1:3, :], lambda r, g: u[r, g, :], lambda r, g: pk[s][r, g, :, :], c3_done,
                         restart=False)

            scores(0, 0)
            square(0)
            fourth(0)
            eighth(0)
            coupling(0)
            coupling2(0)
            inverse(0)
            with pe.Fori(0, NCH) as c:
                with pe.Fori(0, B // 2) as q:
                    for s in range(2):
                        n = c * B + q * 2 + s
                        scores(n + 1, 1 - s)
                        from_state(n, s)
                        square(n + 1)
                        fourth(n + 1)
                        solve(n, s)
                        eighth(n + 1)
                        coupling(n + 1)
                        into_state(n, s)
                        coupling2(n + 1)
                        inverse(n + 1)


def attn_out_phase(nc, tag, o_all, gate_dram, src, dst, wo_dram, vec_dram):
    with ExitStack() as ctx:
        def sb(name, shape, dt=F32):
            return ctx.enter_context(nc.sbuf_tensor(f"{tag}_{name}", shape, dt))

        def sem(name):
            return nc.alloc_semaphore(f"{tag}_{name}")

        w_hi, w_lo = sb("w_hi", [P, KT, C], F32R), sb("w_lo", [P, KT, C], F32R)
        gated = [sb(f"gated{s}", [P, KT, TOK]) for s in range(2)]
        high = [sb(f"high{s}", [P, KT, TOK], F32R) for s in range(2)]
        low = [sb(f"low{s}", [P, KT, TOK], F32R) for s in range(2)]
        x = sb("x", [P, KT, TOK])
        vec = sb("vec", [P, 3, KT])
        head_mean = sb("head_mean", [P, P])
        parts = sb("parts", [P, KT, TPB, 6])
        moments = sb("moments", [P, KT, 2])
        head = sb("head", [P, KT, 2])
        m2, var, std, rstd = (sb(n, [P, KT]) for n in ("m2", "var", "std", "rstd"))
        scale, shift, mu_scale = (sb(n, [P, KT]) for n in ("scale", "shift", "mu_scale"))
        ps_head = ctx.enter_context(nc.psum_tensor(f"{tag}_ps_head", [P, TOK], F32))
        ring = [ctx.enter_context(nc.psum_tensor(f"{tag}_ring{n}", [P, TOK], F32)) for n in range(KT)]

        aggregated = sem("aggregated")
        w_loaded, w_split, ready, pool_step = sem("w_loaded"), sem("w_split"), sem("ready"), sem("pool_step")
        gate_loaded = [sem("gate_loaded0"), sem("gate_loaded1")]
        x_loaded, stored = sem("x_loaded"), sem("stored")
        stat_step, head_summed, rooted, scaled = sem("stat_step"), sem("head_summed"), sem("rooted"), sem("scaled")
        normed, gate_used, high_ready, low_ready = sem("normed"), sem("gate_used"), sem("high_ready"), sem("low_ready")
        projected, added = sem("projected"), sem("added")

        block = ctx.enter_context(nc.Block())

        @block.sync
        def _(sp):
            def load_gate(t, s):
                sp.dma_start(gated[s][:], gate_dram[t, :, :, :]).then_inc(gate_loaded[s], 16)

            sp.dma_start(x[:], wo_dram).then_inc(w_loaded, 16)
            sp.dma_start(vec[:], vec_dram).then_inc(w_loaded, 16)
            for s in range(2):
                load_gate(s, s)
            sp.wait_ge(w_split, 2)
            sp.dma_start(x[:], src[0, :, :, :]).then_inc(x_loaded, 16)

            def slot(t, s, next_gate, next_x):
                if next_gate:
                    sp.wait_ge(low_ready, t + 1)
                    load_gate(t + 2, s)
                sp.wait_ge(added, KT * t + KT)
                sp.dma_start(dst[t, :, :, :], x[:]).then_inc(stored, 16)
                if next_x:
                    sp.wait_ge(stored, 16 * t + 16)
                    sp.dma_start(x[:], src[t + 1, :, :, :]).then_inc(x_loaded, 16)

            with sp.Fori(0, B - 1) as b:
                for s in range(TPB):
                    slot(b * TPB + s, s, True, True)
            for s in range(TPB):
                slot(NT - TPB + s, s, False, s + 1 < TPB)
            sp.wait_ge(stored, 16 * NT)

        @block.vector
        def _(dve):
            STEPS = 12
            count = [w_split, 0]
            dve.wait_ge(w_loaded, 32)
            split_weight(nc, dve, x[:], w_hi[:], w_lo[:], count)
            dve.wait_ge(w_split, count[1])
            nc.vector.memset(parts[:], 0.0).then_inc(ready, 1)
            dve.wait_ge(ready, 1)

            def statistics(b):
                at = STEPS * b

                def step(n):
                    dve.wait_ge(stat_step, at + n)

                for g in range(KT):
                    for half in range(TPB):
                        last = nc.vector.bn_stats(parts[:, g, half, :],
                                                  o_all[:, bass.ds(b, 1), g, half * TOK:(half + 1) * TOK].rearrange("p a t -> p (a t)"))
                last.then_inc(stat_step, 1)
                step(1)
                dve.sem_inc(aggregated, 1)
                for g in range(KT):
                    last = nc.vector.bn_aggr(moments[:, g, :], parts[:, g, :, :].rearrange("p a s -> p (a s)"))
                last.then_inc(stat_step, 1)
                step(2)
                nc.vector.tensor_tensor(m2[:], moments[:, :, 0], moments[:, :, 0], ALU.mult).then_inc(stat_step, 1)
                step(3)
                nc.vector.tensor_tensor(moments[:, :, 1], moments[:, :, 1], m2[:], ALU.add).then_inc(stat_step, 1)
                dve.wait_ge(head_summed, b + 1)
                nc.vector.tensor_copy(head[:].rearrange("p g s -> p (g s)"), ps_head[:, 0:2 * KT]).then_inc(stat_step, 1)
                step(5)
                nc.vector.tensor_tensor(m2[:], head[:, :, 0], head[:, :, 0], ALU.mult).then_inc(stat_step, 1)
                step(6)
                nc.vector.tensor_tensor(var[:], head[:, :, 1], m2[:], ALU.subtract).then_inc(stat_step, 1)
                step(7)
                nc.vector.tensor_scalar_add(var[:], var[:], 1e-5).then_inc(stat_step, 1)
                dve.wait_ge(rooted, b + 1)
                nc.vector.reciprocal(rstd[:], std[:]).then_inc(stat_step, 1)
                step(9)
                dve.wait_ge(normed, TPB * b)
                nc.vector.tensor_tensor(scale[:], rstd[:], vec[:, 0, :], ALU.mult).then_inc(stat_step, 1)
                step(10)
                nc.vector.tensor_tensor(mu_scale[:], head[:, :, 0], scale[:], ALU.mult).then_inc(stat_step, 1)
                step(11)
                nc.vector.tensor_tensor(shift[:], vec[:, 1, :], mu_scale[:], ALU.subtract).then_inc(stat_step, 1)
                step(12)
                nc.vector.tensor_copy(mu_scale[:], scale[:]).then_inc(scaled, 1)
                dve.wait_ge(scaled, b + 1)

            def prepare(t, b, s):
                dve.wait_ge(normed, t + 1)
                dve.wait_ge(gate_loaded[s], 16 * b + 16)
                nc.vector.tensor_tensor(gated[s][:], gated[s][:],
                                        o_all[:, bass.ds(b, 1), :, s * TOK:(s + 1) * TOK].rearrange("p a g t -> p (a g) t"),
                                        ALU.mult).then_inc(gate_used, 1)
                dve.wait_ge(high_ready, t + 1)
                nc.vector.tensor_tensor(low[s][:], gated[s][:], high[s][:].bitcast(F32), ALU.subtract).then_inc(low_ready, 1)

            def finish(t):
                dve.wait_ge(x_loaded, 16 * t + 16)
                for m in range(KT):
                    dve.wait_ge(projected, KT * t + m + 1)
                    nc.vector.scalar_tensor_tensor(out=x[:, m, :], in0=ring[m][:], scalar=vec[:, 2, m:m + 1], in1=x[:, m, :],
                                                   op0=ALU.add, op1=ALU.add).then_inc(added, 1)

            def sequence(b, more):
                prepare(b * TPB + 1, b, 1)
                if more:
                    statistics(b + 1)
                finish(b * TPB)
                if more:
                    prepare(b * TPB + 2, b + 1, 0)
                finish(b * TPB + 1)

            statistics(0)
            prepare(0, 0, 0)
            with dve.Fori(0, B - 1) as b:
                sequence(b, True)
            sequence(B - 1, False)

        @block.gpsimd
        def _(pool):
            view = head_mean[:].rearrange("p (h d) -> p h d", h=HG)
            nc.gpsimd.memset(head_mean[:], 1.0 / HD).then_inc(pool_step, 1)
            pool.wait_ge(pool_step, 1)
            nc.gpsimd.affine_select(out=view, in_=view, compare_op=ALU.is_ge, fill=0.0, base=0,
                                    pattern=[[-HD, HG], [0, HD]], channel_multiplier=1).then_inc(pool_step, 1)
            pool.wait_ge(pool_step, 2)
            nc.gpsimd.affine_select(out=view, in_=view, compare_op=ALU.is_ge, fill=0.0, base=HD - 1,
                                    pattern=[[HD, HG], [0, HD]], channel_multiplier=-1).then_inc(pool_step, 1)

        @block.scalar
        def _(act):
            def root(b):
                act.wait_ge(stat_step, 12 * b + 8)
                nc.scalar.activation(std[:], var[:], ACT.Sqrt).then_inc(rooted, 1)

            def norm(t, b, s):
                act.wait_ge(scaled, b + 1)
                for g in range(KT):
                    view = o_all[:, bass.ds(b, 1), g, s * TOK:(s + 1) * TOK].rearrange("p a t -> p (a t)")
                    last = nc.scalar.activation(view, view, ACT.Identity, bias=shift[:, g:g + 1], scale=scale[:, g:g + 1])
                last.then_inc(normed, 1)
                act.wait_ge(gate_used, t + 1)
                nc.scalar.activation(high[s][:], gated[s][:], ACT.Copy).then_inc(high_ready, 1)

            def sequence(b, more):
                act.wait_ge(projected, KT * TPB * b)
                norm(b * TPB + 1, b, 1)
                if more:
                    root(b + 1)
                    act.wait_ge(projected, KT * TPB * b + KT)
                    norm(b * TPB + 2, b + 1, 0)

            act.wait_ge(ready, 1)
            root(0)
            norm(0, 0, 0)
            with act.Fori(0, B - 1) as b:
                sequence(b, True)
            sequence(B - 1, False)

        @block.tensor
        def _(pe):
            def head_stats(b):
                pe.wait_ge(stat_step, 12 * b + 4)
                nc.tensor.matmul(ps_head[:, 0:2 * KT], head_mean[:], moments[:].rearrange("p g s -> p (g s)"),
                                 start=True, stop=True).then_inc(head_summed, 1)

            def project(t, s):
                pe.wait_ge(low_ready, t + 1)
                pe.wait_ge(added, KT * t)
                for m in range(KT):
                    product(nc, ring[m][:], w_hi, w_lo, m, high[s], low[s]).then_inc(projected, 1)

            def sequence(b, more):
                project(b * TPB, 0)
                if more:
                    head_stats(b + 1)
                project(b * TPB + 1, 1)

            pe.wait_ge(pool_step, 3)
            pe.wait_ge(ready, 1)
            head_stats(0)
            with pe.Fori(0, B - 1) as b:
                sequence(b, True)
            sequence(B - 1, False)


def macaron_block(nc, x, masks, ffn_w, ffn_mu, attn_w, wab, attn_bias, ab_bias, taps, wo, out_vec, out):
    x1 = nc.dram_tensor("x1", [NT, P, KT, TOK], F32).ap()
    x2 = nc.dram_tensor("x2", [NT, P, KT, TOK], F32).ap()
    gate = nc.dram_tensor("gate", [NT, P, KT, TOK], F32).ap()
    streams = nc.dram_tensor("streams", [B * NCH, P, 5 * KT * CH], F32).ap()
    with nc.cleanup_on_exit():
        ffn_phase(nc, "ffn1", x, x1, ffn_w, ffn_mu)
    with nc.cleanup_on_exit():
        attn_in_phase(nc, "ain", x1, streams, gate, attn_w, wab, attn_bias, ab_bias, taps)
    with nc.sbuf_tensor("o_all", [P, B, KT, S], F32) as o_all:
        with nc.cleanup_on_exit():
            recurrence_phase(nc, "rec", streams, masks, o_all)
        with nc.cleanup_on_exit():
            attn_out_phase(nc, "aout", o_all, gate, x1, x2, wo, out_vec)
    with nc.cleanup_on_exit():
        ffn_phase(nc, "ffn2", x2, out, ffn_w, ffn_mu)



def kernel(**inputs):
    import numpy as np
    import concourse.bacc as bacc
    from concourse.bass_utils import run_bass_kernel_spmd

    a = {name: np.asarray(value) for name, value in inputs.items()}
    attn = {name[len("L0_attn_"):]: value for name, value in a.items() if name.startswith("L0_attn_")}
    ffn = {name[len("L0_ffn_"):]: value for name, value in a.items() if name.startswith("L0_ffn_")}

    def tiles(x):
        return np.ascontiguousarray(x.reshape(NT, TOK, KT, P).transpose(0, 3, 2, 1))

    def weight(w):
        return np.ascontiguousarray(w.reshape(KT, P, -1).transpose(1, 0, 2))

    def vectors(vs):
        return np.ascontiguousarray(np.stack(vs).reshape(len(vs), KT, P).transpose(2, 0, 1))

    arrays = {
        "in_x": tiles(attn["x"].reshape(B * S, C)),
        "in_masks": recurrence_masks(),
        **{f"in_ffn_{n}": weight(ffn[f"W_{n}"].T) for n in "rkv"},
        "in_mu": vectors([ffn["mu_r"], ffn["mu_k"]]),
        **{f"in_w{n}": weight(attn[f"W{n}"]) for n in "qkvg"},
        "in_wab": weight(np.concatenate([attn["Wa"], attn["Wb"]], axis=1)),
        "in_bias": vectors([attn[f"b{n}"] for n in "qkvg"]),
        "in_ab_bias": np.ascontiguousarray(np.concatenate([attn["ba"], attn["bb"]])[:, None]),
        "in_taps": np.ascontiguousarray(np.stack([attn[f"{n}_conv"] for n in "qkv"])
                                        .reshape(3, KT, P, TAPS).transpose(2, 0, 1, 3)),
        "in_wo": weight(attn["Wo"]),
        "in_out_vec": vectors([attn["gn_scale"], attn["gn_bias"], attn["bo"]]),
    }
    nc = bacc.Bacc("TRN2", target_bir_lowering=False, num_devices=1)
    d = {name: nc.dram_tensor(name, v.shape, mybir.dt.from_np(v.dtype), kind="ExternalInput").ap() for name, v in arrays.items()}
    out = nc.dram_tensor("out", [NT, P, KT, TOK], F32, kind="ExternalOutput").ap()
    macaron_block(nc, d["in_x"], d["in_masks"], {n: d[f"in_ffn_{n}"] for n in "rkv"}, d["in_mu"],
                  {n: d[f"in_w{n}"] for n in "qkvg"}, d["in_wab"], d["in_bias"], d["in_ab_bias"], d["in_taps"],
                  d["in_wo"], d["in_out_vec"], out)
    r = run_bass_kernel_spmd(nc, [arrays], core_ids=[0])
    got = r.results[0]["out"]
    return np.ascontiguousarray(got.transpose(0, 3, 2, 1)).reshape(B, S, C)
```

```python
from contextlib import ExitStack

import concourse.bass as bass
from concourse import mybir

F32 = mybir.dt.float32
F32R = mybir.dt.float32r
ALU = mybir.AluOpType
ACT = mybir.ActivationFunctionType

P = 128
C = 512
KT = C // P
B, S = 8, 1024
TOK = 512
NT = B * S // TOK
TPB = S // TOK
H, HD = 16, 32
HG = P // HD
CH = 32
NCH = S // CH
CPT = TOK // CH
TAPS = 4
LN_EPS = 1e-5
NQ, NK_, NV, NA, NB = range(5)


def split_weight(nc, dve, staged, hi, lo, done):
    nc.vector.tensor_copy(hi, staged).then_inc(done[0], 1)
    done[1] += 1
    dve.wait_ge(done[0], done[1])
    nc.vector.tensor_tensor(lo, staged, hi.bitcast(F32), ALU.subtract).then_inc(done[0], 1)
    done[1] += 1


def product(nc, out, w_hi, w_lo, m, x_hi, x_lo, width=P, tiles=range(KT)):
    terms = [(w, x) for w, x in ((w_hi, x_hi), (w_hi, x_lo), (w_lo, x_hi))]
    last = None
    for k in tiles:
        for n, (w, x) in enumerate(terms):
            last = nc.tensor.matmul(out, w[:, k, m * width:(m + 1) * width], x[:, k, :],
                                    start=(k == 0 and n == 0), stop=(k == KT - 1 and n == 2))
    return last


def build_identity(nc, pool, ident, done):
    nc.gpsimd.memset(ident, 0.0).then_inc(done, 1)
    pool.wait_ge(done, 1)
    nc.gpsimd.affine_select(out=ident, in_=ident, compare_op=ALU.not_equal, fill=1.0, base=0,
                            pattern=[[-1, P]], channel_multiplier=1).then_inc(done, 1)


def ffn_phase(nc, tag, src, dst, w_dram, mu_dram):
    with ExitStack() as ctx:
        def sb(name, shape, dt=F32):
            return ctx.enter_context(nc.sbuf_tensor(f"{tag}_{name}", shape, dt))

        def sem(name):
            return nc.alloc_semaphore(f"{tag}_{name}")

        W = {n: (sb(f"w{n}h", [P, KT, C], F32R), sb(f"w{n}l", [P, KT, C], F32R)) for n in "rkv"}
        mu = sb("mu", [P, 2, KT])
        mean_w = sb("mean_w", [P, P])
        start_mask = sb("start_mask", [P, NT, KT])
        x = sb("x", [P, KT, TOK])
        xc = sb("xc", [P, KT, TOK])
        xn = sb("xn", [P, KT, TOK + 1])
        diff = sb("diff", [P, KT, TOK])
        mix = {n: sb(f"mix{n}", [P, KT, TOK]) for n in "rk"}
        mix_h = {n: sb(f"mix{n}h", [P, KT, TOK], F32R) for n in "rk"}
        mix_l = {n: sb(f"mix{n}l", [P, KT, TOK], F32R) for n in "rk"}
        gate = sb("gate", [P, KT, TOK])
        act2 = sb("act2", [P, KT, TOK])
        act_h = sb("act_h", [P, KT, TOK], F32R)
        act_l = sb("act_l", [P, KT, TOK], F32R)
        xres = sb("xres", [P, KT, TOK])
        out = sb("out", [P, KT, TOK])
        half = sb("half", [P, 2, TOK])
        half2 = sb("half2", [P, 2, TOK])
        sum1 = sb("sum1", [P, TOK])
        sum2 = sb("sum2", [P, TOK])
        ident, ones = sb("ident", [P, P]), sb("ones", [P, P])
        var_tok, std_tok, rstd_tok = (sb(n, [P, KT]) for n in ("var_tok", "std_tok", "rstd_tok"))
        rstd_diag = sb("rstd_diag", [P, KT, P])
        ps_mean = ctx.enter_context(nc.psum_tensor(f"{tag}_mean", [P, TOK], F32))
        ps_rstd = ctx.enter_context(nc.psum_tensor(f"{tag}_rstd", [P, TOK], F32))
        ring = [ctx.enter_context(nc.psum_tensor(f"{tag}_ring{n}", [P, TOK], F32)) for n in range(6)]

        w_loaded, w_split, consts = sem("w_loaded"), sem("w_split"), sem("consts")
        x_loaded, xres_loaded, stored = sem("x_loaded"), sem("xres_loaded"), sem("stored")
        halved, summed, mean_done, centred = sem("halved"), sem("summed"), sem("mean_done"), sem("centred")
        squared, halved2, summed2, var_done = sem("squared"), sem("halved2"), sem("summed2"), sem("var_done")
        ident_step, inverted, diagonal, spread = sem("ident_step"), sem("inverted"), sem("diagonal"), sem("spread")
        dve_step = sem("dve_step")
        mixed, mix_high, mix_low = sem("mixed"), sem("mix_high"), sem("mix_low")
        r_done, k_done, v_done = sem("r_done"), sem("k_done"), sem("v_done")
        gated, relued, act_sq, act_high, act_low = sem("gated"), sem("relued"), sem("act_sq"), sem("act_high"), sem("act_low")
        var_copied, std_ready = sem("var_copied"), sem("std_ready")
        v_used, out_ready = sem("v_used"), sem("out_ready")

        block = ctx.enter_context(nc.Block())

        @block.sync
        def _(sp):
            for n, stage in zip("rkv", (mix["r"], mix["k"], act2)):
                sp.dma_start(stage[:], w_dram[n]).then_inc(w_loaded, 16)
            sp.dma_start(mu[:], mu_dram).then_inc(w_loaded, 16)
            sp.dma_start(x[:], src[0, :, :, :]).then_inc(x_loaded, 16)

            def load_x(t):
                sp.wait_ge(centred, t)
                sp.dma_start(x[:], src[t, :, :, :]).then_inc(x_loaded, 16)

            def slot(t, ahead):
                sp.wait_ge(out_ready, t)
                sp.dma_start(xres[:], src[t, :, :, :]).then_inc(xres_loaded, 16)
                if ahead:
                    load_x(t + 2)
                sp.wait_ge(out_ready, t + 1)
                sp.dma_start(dst[t, :, :, :], out[:]).then_inc(stored, 16)

            load_x(1)
            with sp.Fori(0, NT - 2) as t:
                slot(t, True)
            slot(NT - 2, False)
            slot(NT - 1, False)
            sp.wait_ge(stored, 16 * NT)

        @block.vector
        def _(dve):
            PER = 2

            nc.vector.memset(mean_w[:], 1.0 / C)
            nc.vector.memset(ones[:], 1.0)
            nc.vector.memset(start_mask[:], 1.0).then_inc(dve_step, 1)
            nc.vector.memset(xn[:, :, TOK:TOK + 1], 0.0)
            dve.wait_ge(dve_step, 1)
            nc.vector.memset(start_mask[:, 0:NT:TPB, :], 0.0).then_inc(dve_step, 1)
            dve.wait_ge(dve_step, 2)
            dve.wait_ge(w_loaded, 16 * 4)
            count = [w_split, 0]
            for n, stage in zip("rkv", (mix["r"], mix["k"], act2)):
                split_weight(nc, dve, stage[:], W[n][0][:], W[n][1][:], count)
            dve.wait_ge(w_split, count[1])
            nc.vector.memset(var_tok[:], 0.0).then_inc(consts, 1)

            def sums(t):
                dve.wait_ge(x_loaded, 16 * t + 16)
                nc.vector.tensor_tensor(half[:], x[:, 0:2, :], x[:, 2:4, :], ALU.add).then_inc(halved, 1)
                dve.wait_ge(halved, t + 1)
                nc.vector.tensor_tensor(sum1[:], half[:, 0, :], half[:, 1, :], ALU.add).then_inc(summed, 1)

            def centre(t):
                dve.wait_ge(mean_done, t + 1)
                nc.vector.tensor_tensor(xc[:], x[:], ps_mean[:].unsqueeze(1).to_broadcast([P, KT, TOK]),
                                        ALU.subtract).then_inc(centred, 1)

            def mixes(t, n, nth):
                for k in range(KT):
                    last = nc.vector.scalar_tensor_tensor(
                        out=mix[n][:, k, :], in0=diff[:, k, :], scalar=mu[:, nth, k:k + 1],
                        in1=xn[:, k, 0:TOK], op0=ALU.mult, op1=ALU.add)
                last.then_inc(mixed, 1)

            def mix_rest(t, n, nth):
                dve.wait_ge(mix_high, 2 * t + nth + 1)
                nc.vector.tensor_tensor(mix_l[n][:], mix[n][:], mix_h[n][:].bitcast(F32), ALU.subtract).then_inc(mix_low, 1)

            def deviations(t):
                dve.wait_ge(var_done, t + 1)
                nc.vector.tensor_scalar_add(var_tok[:], ps_mean[:, 0:KT], LN_EPS).then_inc(var_copied, 1)
                dve.wait_ge(std_ready, t + 1)
                nc.vector.reciprocal(rstd_tok[:], std_tok[:]).then_inc(inverted, 1)
                dve.wait_ge(inverted, t + 1)
                nc.vector.tensor_tensor(rstd_diag[:], ident[:].unsqueeze(1).to_broadcast([P, KT, P]),
                                        rstd_tok[:].unsqueeze(2).to_broadcast([P, KT, P]), ALU.mult).then_inc(diagonal, 1)

            def normalise(t):
                nc.vector.tensor_tensor(xn[:, :, 0:1], xn[:, :, TOK:TOK + 1],
                                        start_mask[:, bass.ds(t, 1), :].rearrange("p a k -> p k a"), ALU.mult).then_inc(dve_step, 1)
                dve.wait_ge(dve_step, PER * t + 3)
                dve.wait_ge(spread, t + 1)
                nc.vector.tensor_tensor(xn[:, :, 1:TOK + 1], xc[:], ps_rstd[:].unsqueeze(1).to_broadcast([P, KT, TOK]),
                                        ALU.mult).then_inc(dve_step, 1)

            def differ(t):
                dve.wait_ge(dve_step, PER * t + 4)
                nc.vector.tensor_tensor(diff[:], xn[:, :, 1:TOK + 1], xn[:, :, 0:TOK], ALU.subtract).then_inc(consts, 1)
                dve.wait_ge(consts, t + 2)

            def act_rest(t, m):
                dve.wait_ge(act_high, KT * t + m + 1)
                nc.vector.tensor_tensor(act_l[:, m, :], act2[:, m, :], act_h[:, m, :].bitcast(F32),
                                        ALU.subtract).then_inc(act_low, 1)

            def slot(t, ahead):
                if ahead:
                    centre(t + 1)
                mix_rest(t, "k", 1)
                if ahead:
                    deviations(t + 1)
                    normalise(t + 1)
                act_rest(t, 0)
                if ahead:
                    differ(t + 1)
                act_rest(t, 1)
                if ahead:
                    mixes(t + 1, "r", 0)
                act_rest(t, 2)
                act_rest(t, 3)
                if ahead:
                    mix_rest(t + 1, "r", 0)
                if ahead == 2:
                    sums(t + 2)
                if ahead:
                    mixes(t + 1, "k", 1)
                for m in range(KT):
                    dve.wait_ge(v_done, KT * t + m + 1)
                    dve.wait_ge(gated, KT * t + m + 1)
                    nc.vector.scalar_tensor_tensor(out=gate[:, m, :], in0=ring[(8 + m) % 6][:], scalar=0.5,
                                                   in1=gate[:, m, :], op0=ALU.mult, op1=ALU.mult).then_inc(v_used, 1)

            dve.wait_ge(ident_step, 2)
            sums(0)
            centre(0)
            deviations(0)
            normalise(0)
            differ(0)
            mixes(0, "r", 0)
            mix_rest(0, "r", 0)
            mixes(0, "k", 1)
            sums(1)
            with dve.Fori(0, NT - 2) as t:
                slot(t, 2)
            slot(NT - 2, 1)
            slot(NT - 1, 0)

        @block.gpsimd
        def _(pool):
            def squares(t):
                pool.wait_ge(squared, t + 1)
                nc.gpsimd.tensor_tensor(half2[:], diff[:, 0:2, :], diff[:, 2:4, :], ALU.add).then_inc(halved2, 1)
                pool.wait_ge(halved2, t + 1)
                nc.gpsimd.tensor_tensor(sum2[:], half2[:, 0, :], half2[:, 1, :], ALU.add).then_inc(summed2, 1)

            def slot(t, more):
                if more:
                    squares(t + 1)
                pool.wait_ge(xres_loaded, 16 * t + 16)
                pool.wait_ge(stored, 16 * t)
                for m in range(KT):
                    pool.wait_ge(v_used, KT * t + m + 1)
                    last = nc.gpsimd.tensor_tensor(out[:, m, :], gate[:, m, :], xres[:, m, :], ALU.add)
                last.then_inc(out_ready, 1)

            build_identity(nc, pool, ident[:], ident_step)
            squares(0)
            with pool.Fori(0, NT - 1) as t:
                slot(t, True)
            slot(NT - 1, False)

        @block.scalar
        def _(act):
            def square(t):
                act.wait_ge(centred, t + 1)
                nc.scalar.activation(diff[:], xc[:], ACT.Square).then_inc(squared, 1)

            def deviation(t):
                act.wait_ge(var_copied, t + 1)
                nc.scalar.activation(std_tok[:], var_tok[:], ACT.Sqrt).then_inc(std_ready, 1)

            def high(t, n, nth):
                act.wait_ge(mixed, 2 * t + nth + 1)
                act.wait_ge((r_done, k_done)[nth], KT * t)
                nc.scalar.activation(mix_h[n][:], mix[n][:], ACT.Copy).then_inc(mix_high, 1)

            def gates(t, m):
                act.wait_ge(r_done, KT * t + m + 1)
                if m == 0:
                    act.wait_ge(out_ready, t)
                nc.scalar.activation(gate[:, m, :], ring[m][:], ACT.Sigmoid).then_inc(gated, 1)

            def activated(t, m):
                act.wait_ge(k_done, KT * t + m + 1)
                act.wait_ge(act_low, KT * t)
                nc.scalar.activation(act2[:, m, :], ring[(4 + m) % 6][:], ACT.Relu).then_inc(relued, 1)
                act.wait_ge(relued, KT * t + m + 1)
                nc.scalar.activation(act2[:, m, :], act2[:, m, :], ACT.Square).then_inc(act_sq, 1)
                act.wait_ge(act_sq, KT * t + m + 1)
                act.wait_ge(v_done, KT * t)
                nc.scalar.activation(act_h[:, m, :], act2[:, m, :], ACT.Copy).then_inc(act_high, 1)

            def slot(t, more):
                if more:
                    square(t + 1)
                for m in range(3):
                    gates(t, m)
                gates(t, 3)
                if more:
                    deviation(t + 1)
                activated(t, 0)
                activated(t, 1)
                activated(t, 2)
                activated(t, 3)
                if more:
                    high(t + 1, "r", 0)
                if more:
                    high(t + 1, "k", 1)

            act.wait_ge(consts, 1)
            square(0)
            deviation(0)
            high(0, "r", 0)
            high(0, "k", 1)
            with act.Fori(0, NT - 1) as t:
                slot(t, True)
            slot(NT - 1, False)

        @block.tensor
        def _(pe):
            def mean(t):
                pe.wait_ge(summed, t + 1)
                nc.tensor.matmul(ps_mean[:], mean_w[:], sum1[:], start=True, stop=True).then_inc(mean_done, 1)

            def var(t):
                pe.wait_ge(summed2, t + 1)
                for j in range(KT):
                    last = nc.tensor.matmul(ps_mean[:, j:j + 1], sum2[:, j * P:(j + 1) * P], mean_w[:, 0:1], start=(j == 0),
                                            stop=True, skip_group_check=True)
                last.then_inc(var_done, 1)

            def spread_rstd(t):
                pe.wait_ge(diagonal, t + 1)
                nc.tensor.matmul(ps_rstd[:], ones[:], rstd_diag[:].rearrange("p j n -> p (j n)"), start=True,
                                 stop=True).then_inc(spread, 1)

            def project(t, n, nth, m, done):
                if m == 0:
                    pe.wait_ge(mix_low, 2 * t + nth + 1)
                if nth == 0:
                    if m == 0:
                        pe.wait_ge(relued, KT * t)
                    if m == 2:
                        pe.wait_ge(v_used, KT * t)
                elif m == 2:
                    pe.wait_ge(gated, KT * t + 2)
                product(nc, ring[(4 * nth + m) % 6][:], *W[n], m, mix_h[n], mix_l[n]).then_inc(done, 1)

            def slot(t, more):
                if more:
                    mean(t + 1)
                for m in range(KT):
                    project(t, "r", 0, m, r_done)
                project(t, "k", 1, 0, k_done)
                if more:
                    var(t + 1)
                project(t, "k", 1, 1, k_done)
                if more:
                    spread_rstd(t + 1)
                for m in range(2, KT):
                    project(t, "k", 1, m, k_done)
                pe.wait_ge(gated, KT * t + KT)
                pe.wait_ge(relued, KT * t + 2)
                for k in range(2):
                    pe.wait_ge(act_low, KT * t + k + 1)
                    for m in range(KT):
                        product(nc, ring[(8 + m) % 6][:], *W["v"], m, act_h, act_l, tiles=(k,))
                pe.wait_ge(act_low, KT * t + KT)
                for m in range(KT):
                    product(nc, ring[(8 + m) % 6][:], *W["v"], m, act_h, act_l, tiles=(2, 3)).then_inc(v_done, 1)

            pe.wait_ge(consts, 1)
            pe.wait_ge(ident_step, 2)
            mean(0)
            var(0)
            spread_rstd(0)
            with pe.Fori(0, NT - 1) as t:
                slot(t, True)
            slot(NT - 1, False)


def attn_in_phase(nc, tag, src, streams, gate_dram, w_dram, wab_dram, bias_dram, ab_bias_dram, conv_dram):
    with ExitStack() as ctx:
        def sb(name, shape, dt=F32):
            return ctx.enter_context(nc.sbuf_tensor(f"{tag}_{name}", shape, dt))

        def pb(name):
            return ctx.enter_context(nc.psum_tensor(f"{tag}_ps_{name}", [P, TOK], F32))

        def sem(name):
            return nc.alloc_semaphore(f"{tag}_{name}")

        W = {n: (sb(f"w{n}h", [P, KT, C], F32R), sb(f"w{n}l", [P, KT, C], F32R)) for n in "qkvg"}
        wab_h, wab_l = sb("wab_h", [P, KT, P], F32R), sb("wab_l", [P, KT, P], F32R)
        bias = sb("bias", [P, 4, KT])
        ab_bias = sb("ab_bias", [P, 1])
        taps = sb("taps", [P, 3, KT, TAPS])
        mean_w = sb("mean_w", [P, P])
        start_mask = sb("start_mask", [P, NT, 3 * KT, TAPS - 1])
        head_sum = sb("head_sum", [P, 2 * KT, P])
        spread_f = sb("spread_f", [P, P])
        spread = sb("spread", [P, 4 * KT, P], F32R)
        x = sb("x", [P, KT, TOK])
        xc = sb("xc", [P, KT, TOK])
        xh, xl = sb("xh", [P, KT, TOK], F32R), sb("xl", [P, KT, TOK], F32R)
        sq = sb("sq", [P, 4, TOK])
        half, half2 = sb("half", [P, 2, TOK]), sb("half2", [P, 2, TOK])
        sum1, sum2 = sb("sum1", [P, TOK]), sb("sum2", [P, TOK])
        ident, ones = sb("ident", [P, P]), sb("ones", [P, P])
        var_tok, std_tok, rstd_tok = (sb(n, [P, KT]) for n in ("var_tok", "std_tok", "rstd_tok"))
        rstd_diag = sb("rstd_diag", [P, KT, P])
        padded = [sb(f"padded{r}", [P, TOK + TAPS - 1]) for r in range(3)]
        tail = sb("tail", [P, 3 * KT, TAPS - 1])
        bias_tap = sb("bias_tap", [P, 3 * KT])
        term = sb("term", [P, TOK])
        conv = [sb(f"conv{r}", [P, TOK]) for r in range(3)]
        rows = sb("rows", [P, TOK])
        rows_h, rows_l = sb("rows_h", [P, TOK], F32R), sb("rows_l", [P, TOK], F32R)
        buf = sb("buf", [P, CPT, 5, KT, CH])
        gate = sb("gate", [P, KT, TOK])
        flat = buf[:].rearrange("p c s g i -> p (c s g i)")
        stage = [flat[:, n * KT * C:(n + 1) * KT * C].rearrange("p (k n) -> p k n", k=KT) for n in range(4)]
        ps_mean, ps_rstd, ps_rows = pb("mean"), pb("rstd"), pb("rows")
        ring = [pb(f"ring{n}") for n in range(4)]

        w_loaded, w_split, padded_w = sem("w_loaded"), sem("w_split"), sem("padded_w")
        consts_pool, sel_step, ready = sem("consts_pool"), sem("sel_step"), sem("ready")
        x_loaded, stored, gate_stored = sem("x_loaded"), sem("stored"), sem("gate_stored")
        halved, summed, mean_done, centred = sem("halved"), sem("summed"), sem("mean_done"), sem("centred")
        squared, halved2, summed2, var_done = sem("squared"), sem("halved2"), sem("summed2"), sem("var_done")
        ident_step, inverted, diagonal, spread_done = sem("ident_step"), sem("inverted"), sem("diagonal"), sem("spread_done")
        var_copied, std_ready, norm_step = sem("var_copied"), sem("std_ready"), sem("norm_step")
        x_high, x_low = sem("x_high"), sem("x_low")
        group_done, ab_done, sigmoided = sem("group_done"), sem("ab_done"), sem("sigmoided")
        biased, conv_step, silued = sem("biased"), sem("conv_step"), sem("silued")
        pool_conv, tails_masked, pool_turns = sem("pool_conv"), sem("tails_masked"), sem("pool_turns")
        q_squared, heads_summed, rooted = sem("q_squared"), sem("heads_summed"), sem("rooted")
        rows_step = sem("rows_step")
        ring_act, ring_dve, gate_ready = sem("ring_act"), sem("ring_dve"), sem("gate_ready")

        D_STEPS, D_UNITS, P_STEPS, P_UNITS = TAPS + 1, 8, 2 * TAPS, 4

        def dve_unit(u):
            return u // 3 * 2 + u % 3

        def wait_convolved(eng, t, u):
            if u % 3 == 2:
                eng.wait_ge(pool_conv, P_STEPS * (P_UNITS * t + u // 3 + 1))
            else:
                eng.wait_ge(conv_step, D_STEPS * (D_UNITS * t + dve_unit(u) + 1))

        block = ctx.enter_context(nc.Block())

        @block.sync
        def _(sp):
            for n, s in zip("qkvg", stage):
                sp.dma_start(s, w_dram[n]).then_inc(w_loaded, 16)
            for dst, s in ((bias[:], bias_dram), (taps[:], conv_dram)):
                sp.dma_start(dst, s).then_inc(w_loaded, 16)
            sp.wait_ge(padded_w, 2)
            sp.dma_start(xc[:, :, 0:2 * H], wab_dram).then_inc(w_loaded, 16)
            sp.dma_start(ab_bias[0:2 * H, :], ab_bias_dram).then_inc(w_loaded, 16)
            sp.dma_start(x[:], src[0, :, :, :]).then_inc(x_loaded, 16)

            def load_x(t):
                sp.wait_ge(centred, t)
                sp.dma_start(x[:], src[t, :, :, :]).then_inc(x_loaded, 16)

            def slot(t, ahead):
                if ahead:
                    load_x(t + 2)
                sp.wait_ge(gate_ready, KT * t + KT)
                sp.dma_start(gate_dram[t, :, :, :], gate[:]).then_inc(gate_stored, 16)
                sp.wait_ge(ring_act, 8 * t + 8)
                sp.wait_ge(ring_dve, 8 * t + 8)
                sp.dma_start(streams[bass.ds(t * CPT, CPT), :, :].rearrange("c p f -> p c f"),
                             buf[:].rearrange("p c s g i -> p c (s g i)")).then_inc(stored, 16)

            load_x(1)
            with sp.Fori(0, NT - 2) as t:
                slot(t, True)
            slot(NT - 2, False)
            slot(NT - 1, False)
            sp.wait_ge(stored, 16 * NT)
            sp.wait_ge(gate_stored, 16 * NT)

        @block.vector
        def _(dve):
            ROWS = 4
            nc.vector.memset(xc[:], 0.0).then_inc(padded_w, 1)
            nc.vector.memset(ab_bias[:], 0.0).then_inc(padded_w, 1)
            nc.vector.memset(mean_w[:], 1.0 / C)
            nc.vector.memset(ones[:], 1.0)
            nc.vector.memset(tail[:], 0.0)
            nc.vector.memset(rows[:], 0.0)
            nc.vector.memset(start_mask[:], 1.0).then_inc(w_split, 1)
            dve.wait_ge(w_split, 1)
            nc.vector.memset(start_mask[:, 0:NT:TPB, :, :], 0.0)
            dve.wait_ge(w_loaded, 16 * 8)
            nc.vector.tensor_tensor(bias_tap[:].rearrange("p (j k) -> p j k", k=KT), bias[:, 0:3, :], taps[:, :, :, TAPS - 1],
                                    ALU.mult)
            count = [w_split, 1]
            for n, s in zip("qkvg", stage):
                split_weight(nc, dve, s, W[n][0][:], W[n][1][:], count)
            split_weight(nc, dve, xc[:, :, 0:P], wab_h[:], wab_l[:], count)
            dve.wait_ge(w_split, count[1])
            nc.vector.tensor_copy(rows_h[:], rows[:])
            nc.vector.tensor_copy(rows_l[:], rows[:]).then_inc(ready, 1)

            def sums(t):
                dve.wait_ge(x_loaded, 16 * t + 16)
                nc.vector.tensor_tensor(half[:], x[:, 0:2, :], x[:, 2:4, :], ALU.add).then_inc(halved, 1)
                dve.wait_ge(halved, t + 1)
                nc.vector.tensor_tensor(sum1[:], half[:, 0, :], half[:, 1, :], ALU.add).then_inc(summed, 1)

            def centre(t):
                dve.wait_ge(mean_done, t + 1)
                nc.vector.tensor_tensor(xc[:], x[:], ps_mean[:].unsqueeze(1).to_broadcast([P, KT, TOK]),
                                        ALU.subtract).then_inc(centred, 1)

            def deviations(t):
                dve.wait_ge(var_done, t + 1)
                nc.vector.tensor_scalar_add(var_tok[:], ps_mean[:, 0:KT], LN_EPS).then_inc(var_copied, 1)
                dve.wait_ge(std_ready, t + 1)
                nc.vector.reciprocal(rstd_tok[:], std_tok[:]).then_inc(inverted, 1)
                dve.wait_ge(inverted, t + 1)
                nc.vector.tensor_tensor(rstd_diag[:], ident[:].unsqueeze(1).to_broadcast([P, KT, P]),
                                        rstd_tok[:].unsqueeze(2).to_broadcast([P, KT, P]), ALU.mult).then_inc(diagonal, 1)

            def normalise(t):
                dve.wait_ge(spread_done, t + 1)
                nc.vector.tensor_tensor(xc[:], xc[:], ps_rstd[:].unsqueeze(1).to_broadcast([P, KT, TOK]),
                                        ALU.mult).then_inc(norm_step, 1)

            def low(t):
                dve.wait_ge(x_high, t + 1)
                nc.vector.tensor_tensor(xl[:], xc[:], xh[:].bitcast(F32), ALU.subtract).then_inc(x_low, 1)

            def mask_tails(t):
                dve.wait_ge(conv_step, D_STEPS * D_UNITS * t)
                dve.wait_ge(pool_conv, P_STEPS * P_UNITS * t)
                nc.vector.tensor_tensor(tail[:].unsqueeze(1), tail[:].unsqueeze(1), start_mask[:, bass.ds(t, 1), :, :],
                                        ALU.mult).then_inc(tails_masked, 1)
                dve.wait_ge(tails_masked, t + 1)

            def convolve(t, u):
                pad, out = padded[u % 3], conv[u % 3]
                at = D_STEPS * (D_UNITS * t + dve_unit(u))
                dve.wait_ge(biased, 12 * t + u + 1)
                nc.vector.tensor_copy(pad[:, 0:TAPS - 1], tail[:, u, :]).then_inc(conv_step, 1)
                dve.wait_ge(conv_step, at + 1)
                nc.vector.tensor_copy(tail[:, u, :], pad[:, TOK:TOK + TAPS - 1]).then_inc(conv_step, 1)
                for n in range(TAPS - 1):
                    dve.wait_ge(conv_step, at + 2 + n)
                    nc.vector.scalar_tensor_tensor(out=out[:], in0=pad[:, n:n + TOK], scalar=taps[:, u // KT, u % KT, n:n + 1],
                                                   in1=out[:], op0=ALU.mult, op1=ALU.add).then_inc(conv_step, 1)

            def norms(t):
                dve.wait_ge(rooted, t + 1)
                nc.vector.tensor_scalar_add(rows[2 * H:4 * H, :], rows[2 * H:4 * H, :], 1e-6).then_inc(rows_step, 1)
                dve.wait_ge(rows_step, ROWS * t + 1)
                nc.vector.reciprocal(rows[2 * H:4 * H, :], rows[2 * H:4 * H, :]).then_inc(rows_step, 1)
                dve.wait_ge(rows_step, ROWS * t + 2)
                dve.wait_ge(sigmoided, t + 1)
                nc.vector.tensor_copy(rows_h[0:4 * H, :], rows[0:4 * H, :]).then_inc(rows_step, 1)
                dve.wait_ge(rows_step, ROWS * t + 3)
                nc.vector.tensor_tensor(rows_l[0:4 * H, :], rows[0:4 * H, :], rows_h[0:4 * H, :].bitcast(F32),
                                        ALU.subtract).then_inc(rows_step, 1)

            def slot(t, ahead):
                mask_tails(t)
                if ahead:
                    centre(t + 1)
                for u in range(12):
                    if u % 3 < 2:
                        convolve(t, u)
                if ahead:
                    deviations(t + 1)
                norms(t)
                if ahead:
                    normalise(t + 1)
                for n in range(2 * KT):
                    if ahead and n == 2:
                        low(t + 1)
                    dve.wait_ge(group_done, 32 * t + 16 + 2 * n + 2)
                    j, g = divmod(n, KT)
                    view = buf[:, :, j, g, :]
                    nc.vector.tensor_tensor(view, view, ring[(2 * n + 1) % 4][:].rearrange("p (c i) -> p c i", i=CH),
                                            ALU.mult).then_inc(ring_dve, 1)
                if ahead == 2:
                    sums(t + 2)

            dve.wait_ge(ident_step, 2)
            sums(0)
            centre(0)
            deviations(0)
            normalise(0)
            low(0)
            sums(1)
            with dve.Fori(0, NT - 2) as t:
                slot(t, 2)
            slot(NT - 2, 1)
            slot(NT - 1, 0)

        @block.gpsimd
        def _(pool):
            build_identity(nc, pool, ident[:], ident_step)
            nc.gpsimd.memset(head_sum[:], 1.0).then_inc(sel_step, 1)
            pool.wait_ge(sel_step, 1)
            pattern = [[HG * HD, 2 * KT], [-HD, P]]
            base = 2 * H * HD
            nc.gpsimd.affine_select(out=head_sum[:], in_=head_sum[:], compare_op=ALU.is_ge, fill=0.0, base=base,
                                    pattern=pattern, channel_multiplier=1).then_inc(sel_step, 1)
            pool.wait_ge(sel_step, 2)
            nc.gpsimd.affine_select(out=head_sum[:], in_=head_sum[:], compare_op=ALU.is_ge, fill=0.0, base=HD - 1 - base,
                                    pattern=[[-s, n] for s, n in pattern], channel_multiplier=-1).then_inc(sel_step, 1)
            for n in range(4 * KT):
                nc.gpsimd.memset(spread_f[:], 0.0).then_inc(sel_step, 1)
                pool.wait_ge(sel_step, 3 * n + 4)
                view = spread_f[:].rearrange("p (h d) -> p h d", h=HG)
                nc.gpsimd.affine_select(out=view, in_=view, compare_op=ALU.not_equal, fill=1.0, base=-HG * n,
                                        pattern=[[-1, HG], [0, HD]], channel_multiplier=1).then_inc(sel_step, 1)
                pool.wait_ge(sel_step, 3 * n + 5)
                last = nc.gpsimd.tensor_copy(spread[:, n, :], spread_f[:])
                last.then_inc(sel_step, 1)
                pool.wait_ge(sel_step, 3 * n + 6)
            nc.gpsimd.memset(half2[:, 0, 0:1], 0.0).then_inc(consts_pool, 1)

            def squares(t):
                pool.wait_ge(squared, t + 1)
                nc.gpsimd.tensor_tensor(half2[:], gate[:, 0:2, :], gate[:, 2:4, :], ALU.add).then_inc(halved2, 1)
                pool.wait_ge(halved2, t + 1)
                nc.gpsimd.tensor_tensor(sum2[:], half2[:, 0, :], half2[:, 1, :], ALU.add).then_inc(summed2, 1)

            def convolve(t, u):
                at = P_STEPS * (P_UNITS * t + u // 3)
                pad, out = padded[2], conv[2]

                def turn():
                    pool.sem_inc(pool_turns, 1)

                pool.wait_ge(biased, 12 * t + u + 1)
                turn()
                nc.gpsimd.tensor_copy(pad[:, 0:TAPS - 1], tail[:, u, :]).then_inc(pool_conv, 1)
                pool.wait_ge(pool_conv, at + 1)
                turn()
                nc.gpsimd.tensor_copy(tail[:, u, :], pad[:, TOK:TOK + TAPS - 1]).then_inc(pool_conv, 1)
                for n in range(TAPS - 1):
                    pool.wait_ge(pool_conv, at + 2 + 2 * n)
                    turn()
                    nc.gpsimd.tensor_scalar(term[:], pad[:, n:n + TOK], taps[:, u // KT, u % KT, n:n + 1], 1.0,
                                            ALU.mult, ALU.mult).then_inc(pool_conv, 1)
                    pool.wait_ge(pool_conv, at + 3 + 2 * n)
                    nc.gpsimd.tensor_tensor(out[:], out[:], term[:], ALU.add).then_inc(pool_conv, 1)

            def slot(t, more):
                pool.wait_ge(tails_masked, t + 1)
                convolve(t, 2)
                if more:
                    squares(t + 1)
                for u in (5, 8, 11):
                    convolve(t, u)

            squares(0)
            with pool.Fori(0, NT - 1) as t:
                slot(t, True)
            slot(NT - 1, False)

        @block.scalar
        def _(act):
            def square(t):
                act.wait_ge(centred, t + 1)
                nc.scalar.activation(gate[:], xc[:], ACT.Square).then_inc(squared, 1)

            def deviation(t):
                act.wait_ge(var_copied, t + 1)
                nc.scalar.activation(std_tok[:], var_tok[:], ACT.Sqrt).then_inc(std_ready, 1)

            def high(t):
                act.wait_ge(norm_step, t + 1)
                nc.scalar.activation(xh[:], xc[:], ACT.Copy).then_inc(x_high, 1)

            def shift(t, u):
                act.wait_ge(group_done, 32 * t + u + 1)
                if u >= 3:
                    wait_convolved(act, t, u - 3)
                nc.scalar.activation(padded[u % 3][:, TAPS - 1:], ring[u % 4][:], ACT.Identity,
                                     bias=bias[:, u // KT, u % KT:u % KT + 1])
                if u < 3:
                    act.wait_ge(silued, 12 * t)
                else:
                    act.wait_ge(silued, 12 * t + u - 2)
                nc.scalar.activation(conv[u % 3][:], ring[u % 4][:], ACT.Identity, bias=bias_tap[:, u:u + 1],
                                     scale=taps[:, u // KT, u % KT, TAPS - 1:TAPS]).then_inc(biased, 1)

            def silu(t, u):
                j, m = divmod(u, KT)
                wait_convolved(act, t, u)
                if u == 0:
                    act.wait_ge(stored, 16 * t)
                view = buf[:, :, j, m, :]
                nc.scalar.activation(view, conv[u % 3][:].rearrange("p (c i) -> p c i", i=CH), ACT.Silu).then_inc(silued, 1)
                if j < 2:
                    act.wait_ge(silued, 12 * t + u + 1)
                    if u < 4:
                        act.wait_ge(heads_summed, 8 * t)
                    else:
                        act.wait_ge(heads_summed, 8 * t + u - 3)
                    nc.scalar.activation(sq[:, u % 4, :].rearrange("p (c i) -> p c i", i=CH), view,
                                         ACT.Square).then_inc(q_squared, 1)

            def rows_copy(t, n):
                act.wait_ge(group_done, 32 * t + 16 + 2 * n + 1)
                nc.scalar.activation(buf[:, :, NA + n // KT, n % KT, :],
                                     ring[2 * n % 4][:].rearrange("p (c i) -> p c i", i=CH), ACT.Copy).then_inc(ring_act, 1)

            def slot(t, more):
                act.wait_ge(ab_done, t + 1)
                act.wait_ge(rows_step, 4 * t)
                nc.scalar.activation(rows[0:2 * H, :], ps_rows[0:2 * H, :], ACT.Sigmoid,
                                     bias=ab_bias[0:2 * H, :]).then_inc(sigmoided, 1)
                if more:
                    act.wait_ge(gate_stored, 16 * t)
                    square(t + 1)
                for u in range(12):
                    shift(t, u)
                    if u > 1:
                        silu(t, u - 2)
                if more:
                    deviation(t + 1)
                act.wait_ge(heads_summed, 8 * t + 8)
                nc.scalar.activation(rows[2 * H:4 * H, :], ps_rows[2 * H:4 * H, :], ACT.Sqrt).then_inc(rooted, 1)
                if more:
                    act.wait_ge(halved2, t + 2)
                act.wait_ge(gate_stored, 16 * t)
                silu(t, 10)
                for m in range(KT):
                    if m == 2:
                        silu(t, 11)
                    act.wait_ge(group_done, 32 * t + 12 + m + 1)
                    nc.scalar.activation(gate[:, m, :], ring[m][:], ACT.Silu, bias=bias[:, 3, m:m + 1]).then_inc(gate_ready, 1)
                rows_copy(t, 0)
                if more:
                    high(t + 1)
                for n in range(1, 2 * KT):
                    rows_copy(t, n)

            act.wait_ge(ready, 1)
            act.wait_ge(consts_pool, 1)
            square(0)
            deviation(0)
            high(0)
            with act.Fori(0, NT - 1) as t:
                slot(t, True)
            slot(NT - 1, False)

        @block.tensor
        def _(pe):
            def mean(t):
                pe.wait_ge(summed, t + 1)
                nc.tensor.matmul(ps_mean[:], mean_w[:], sum1[:], start=True, stop=True).then_inc(mean_done, 1)

            def var(t):
                pe.wait_ge(summed2, t + 1)
                for j in range(KT):
                    last = nc.tensor.matmul(ps_mean[:, j:j + 1], sum2[:, j * P:(j + 1) * P], mean_w[:, 0:1], start=(j == 0),
                                            stop=True, skip_group_check=True)
                last.then_inc(var_done, 1)

            def spread_rstd(t):
                pe.wait_ge(diagonal, t + 1)
                nc.tensor.matmul(ps_rstd[:], ones[:], rstd_diag[:].rearrange("p j n -> p (j n)"), start=True,
                                 stop=True).then_inc(spread_done, 1)

            def head_sums(t, n):
                pe.wait_ge(q_squared, 8 * t + n + 1)
                if n == 0:
                    pe.wait_ge(sigmoided, t + 1)
                nc.tensor.matmul(ps_rows[:], head_sum[:, n, :], sq[:, n % 4, :], start=(n == 0),
                                 stop=(n == 7)).then_inc(heads_summed, 1)

            def slot(t, more):
                if more:
                    mean(t + 1)
                pe.wait_ge(x_low, t + 1)
                pe.wait_ge(rooted, t)
                product(nc, ps_rows[:], wab_h, wab_l, 0, xh, xl).then_inc(ab_done, 1)
                for u in range(16):
                    j, m = divmod(u, KT)
                    if u < 4:
                        if u == 0:
                            pe.wait_ge(ring_dve, 8 * t)
                            pe.wait_ge(ring_act, 8 * t)
                    else:
                        pe.wait_ge(biased, 12 * t + u - 3)
                    product(nc, ring[u % 4][:], *W["qkvg"[j]], m, xh, xl).then_inc(group_done, 1)
                    if 4 <= u < 12:
                        head_sums(t, u - 4)
                    if more and u == 11:
                        var(t + 1)
                    if more and u == 14:
                        spread_rstd(t + 1)
                for n in range(16):
                    if n < 4:
                        pe.wait_ge(gate_ready, 4 * t + n + 1)
                    else:
                        pe.wait_ge((ring_act, ring_dve)[n % 2], 8 * t + n // 2 - 1)
                    if n == 0:
                        pe.wait_ge(rows_step, 4 * t + 4)
                    which = spread[:, n // 2 + n % 2 * 2 * KT, :]
                    nc.tensor.matmul(ring[n % 4][:], which, rows_h[:], start=True, stop=False)
                    nc.tensor.matmul(ring[n % 4][:], which, rows_l[:], start=False, stop=True).then_inc(group_done, 1)

            pe.wait_ge(ready, 1)
            pe.wait_ge(consts_pool, 1)
            pe.wait_ge(ident_step, 2)
            mean(0)
            var(0)
            spread_rstd(0)
            with pe.Fori(0, NT - 1) as t:
                slot(t, True)
            slot(NT - 1, False)


DELTA, NOT_FIRST, FIRST, IN_BLOCK, OFF_BLOCK = range(5)
BLOCK = 4
TURN = 4


def recurrence_masks():
    import numpy as np
    j, i = np.arange(P)[:, None] % CH, np.arange(CH)[None, :]
    kinds = [i == j, (i > 0) & (j >= 0), (i == 0) & (j >= 0),
             (i > j) & (i // BLOCK == j // BLOCK), (i > j) & (i // BLOCK != j // BLOCK)]
    return np.stack([np.tile(k, (1, KT)) for k in kinds], axis=1).astype(np.float32)


def recurrence_phase(nc, tag, streams, masks_dram, o_all):
    with ExitStack() as ctx:
        def sb(name, shape, dt=F32):
            return ctx.enter_context(nc.sbuf_tensor(f"{tag}_{name}", shape, dt))

        def pb(name, width):
            t = ctx.enter_context(nc.psum_tensor(f"{tag}_ps_{name}", [P, KT * 128], F32))
            return t[:].rearrange("p (g x) -> p g x", g=KT)[:, :, 0:width * CH].rearrange("p g (w i) -> p g w i", i=CH)

        def sem(name):
            return nc.alloc_semaphore(f"{tag}_{name}")

        tile = [P, KT, CH]
        pair = [P, 2, KT, CH]
        masks = sb("masks", [P, 5, KT * CH])
        inb = [sb(f"inb{s}", [P, 5, KT, CH]) for s in range(2)]
        vt = [sb(f"vt{s}", tile) for s in range(2)]
        kb = [sb(f"kb{s}", tile) for s in range(2)]
        decays = sb("decays", [P, 2, KT * CH])
        dmat, gam, kb_t = sb("dmat", tile), sb("gam", tile), sb("kb_t", tile)
        d_pair = sb("d_pair", pair)
        gqk = [sb(f"gqk{s}", pair) for s in range(TURN)]
        kwp = [sb(f"kwp{s}", pair) for s in range(TURN)]
        g_last = [sb(f"g_last{s}", [P, KT, 1]) for s in range(TURN)]
        a_pair, a_in_t, a2_t = sb("a_pair", pair), sb("a_in_t", tile), sb("a2_t", tile)
        tg = sb("tg", pair)
        tf, f_t = sb("tf", pair), sb("f_t", tile)
        yf, f2_t = sb("yf", pair), sb("f2_t", tile)
        f4_t, y2, inv_t = sb("f4_t", tile), sb("y2", tile), sb("inv_t", tile)
        state = sb("state", [P, B, KT, CH])
        s_cur, s_cur_t, s_decayed = sb("s_cur", tile), sb("s_cur_t", tile), sb("s_decayed", tile)
        z_t, z, u = sb("z_t", tile), sb("z", tile), sb("u", tile)
        ps_scores, ps_a, ps_tg, ps_f, ps_f2 = pb("scores", 2), pb("a", 2), pb("tg", 2), pb("f", 2), pb("f2", 2)
        ps_f4, ps_u = pb("f4", 1), pb("u", 1)
        ps_chain = pb("chain", 3)

        masks_loaded, state_zero, pe_turns = sem("masks_loaded"), sem("state_zero"), sem("pe_turns")
        in_loaded, v_loaded = [sem("in0"), sem("in1")], [sem("v0"), sem("v1")]
        kb_ready, decays_ready, dmat_ready, gam_ready = sem("kb"), sem("decays"), sem("dmat"), sem("gam")
        dpair_ready, kbt_ready, gqk_ready, kw_ready = sem("dpair"), sem("kbt"), sem("gqk"), sem("kw")
        scores_done, apair_ready, aint_ready, pt_ready, t2_ready = (
            sem("scores_done"), sem("apair"), sem("aint"), sem("pt"), sem("t2"))
        a_squared, a2t_ready, g_ready = sem("a_squared"), sem("a2t"), sem("g")
        tg_done, tf_ready, ft_ready = sem("tg_done"), sem("tf"), sem("ft")
        f_squared, y1_ready, f2t_ready, f2_ready = sem("f_squared"), sem("y1"), sem("f2t"), sem("f2")
        f2_squared, f4t_ready, y2_ready = sem("f2_squared"), sem("f4t"), sem("y2r")
        f4_done, inv_ready = sem("f4_done"), sem("inv")
        cur_ready, curt_ready, sdec_ready = sem("cur"), sem("curt"), sem("sdec")
        read_done, zt_ready, z_ready = sem("read_done"), sem("zt"), sem("zr")
        solved, u_ready, wrote, o_ready, state_ready = sem("solved"), sem("ur"), sem("wrote"), sem("o"), sem("state_new")

        def both(bank):
            return bank[:, :, 0:2, :].rearrange("p g w i -> p w g i")

        block = ctx.enter_context(nc.Block())

        @block.sync
        def _(sp):
            def load_in(s, b, c):
                sp.dma_start(inb[s][:].rearrange("p s g i -> p (s g i)"),
                             streams[bass.ds(b * NCH + c, 1), :, :].rearrange("c p f -> p (c f)")).then_inc(in_loaded[s], 16)

            def load_v(s, b, c):
                sp.dma_start(vt[s][:].rearrange("p g i -> p (g i)"),
                             streams[bass.ds(b * NCH + c, 1), :, NV * KT * CH:(NV + 1) * KT * CH].rearrange("c p f -> p (c f)")
                             ).then_inc(v_loaded[s], 16)

            def reload_in(m, s, b, c):
                sp.wait_ge(scores_done, m - 1)
                sp.wait_ge(gqk_ready, m - 1)
                load_in(s, b, c)

            sp.dma_start(masks[:], masks_dram).then_inc(masks_loaded, 16)
            for s in range(2):
                load_in(s, s, 0)
                load_v(s, s, 0)
            for m in (2, 3):
                reload_in(m, m % 2, m, 0)
            with sp.Fori(0, NCH) as c:
                with sp.Fori(0, B // TURN) as q:
                    for s in range(TURN):
                        n = c * B + q * TURN + s
                        reload_in(n + 4, s % 2, (q + 1) % 2 * TURN + s, (c + q) % NCH)
                        sp.wait_ge(zt_ready, n + 1)
                        if s < TURN - 2:
                            load_v(s % 2, q * TURN + s + 2, c)
                        else:
                            load_v(s % 2, (q + 1) % 2 * TURN + s + 2 - TURN, (c + q) % NCH)
            for s in range(2):
                sp.wait_ge(in_loaded[s], 16 * (NCH * B + 4) // 2)
                sp.wait_ge(v_loaded[s], 16 * (NCH * B + 2) // 2)

        @block.gpsimd
        def _(pool):
            mul = ALU.mult

            def scale(m, s, loads):
                pool.wait_ge(in_loaded[s % 2], 16 * loads)
                if not isinstance(m, int) or m > 1:
                    pool.wait_ge(scores_done, m - 1)
                    pool.wait_ge(kbt_ready, m - 1)
                nc.gpsimd.tensor_tensor(kb[s % 2][:], inb[s % 2][:, NK_], inb[s % 2][:, NB], mul).then_inc(kb_ready, 1)
                pool.wait_ge(gam_ready, m)
                pool.wait_ge(dmat_ready, m)
                nc.gpsimd.tensor_tensor(decays[:], inb[s % 2][:, NA:NA + 1].rearrange("p a g i -> p a (g i)").to_broadcast([P, 2, KT * CH]),
                                        masks[:, NOT_FIRST:FIRST + 1, :], mul).then_inc(decays_ready, 1)

            def scale_more(m, s):
                pool.wait_ge(dmat_ready, m + 1)
                pool.wait_ge(apair_ready, m)
                nc.gpsimd.tensor_tensor(d_pair[:], dmat[:].unsqueeze(1).to_broadcast(pair),
                                        masks[:, IN_BLOCK:OFF_BLOCK + 1, :].rearrange("p w (g i) -> p w g i", i=CH),
                                        mul).then_inc(dpair_ready, 1)
                pool.wait_ge(gam_ready, m + 1)
                if not isinstance(m, int) or m > 2:
                    pool.wait_ge(sdec_ready, m - 3)
                    pool.wait_ge(read_done, m - 3)
                nc.gpsimd.tensor_tensor(gqk[s][:], inb[s % 2][:, NQ:NK_ + 1], gam[:].unsqueeze(1).to_broadcast(pair), mul)
                nc.gpsimd.tensor_copy(g_last[s][:], gam[:, :, CH - 1:CH]).then_inc(gqk_ready, 1)
                pool.wait_ge(kbt_ready, m + 1)
                if not isinstance(m, int) or m > 2:
                    pool.wait_ge(wrote, m - 3)
                nc.gpsimd.tensor_tensor(kwp[s][:, 0], kb_t[:], dmat[:, :, CH - 1:CH].to_broadcast(tile), mul).then_inc(kw_ready, 1)

            def first_inverse(m):
                pool.wait_ge(apair_ready, m + 1)
                pool.wait_ge(tf_ready, m)
                nc.gpsimd.tensor_tensor(tg[:, 0], masks[:, DELTA, :].rearrange("p (g i) -> p g i", i=CH), a_pair[:, 0],
                                        ALU.subtract).then_inc(t2_ready, 1)

            def decay_state(n, s):
                pool.wait_ge(cur_ready, n + 1)
                pool.wait_ge(state_ready, n)
                pool.wait_ge(gqk_ready, n + 1)
                nc.gpsimd.tensor_tensor(s_decayed[:], s_cur[:], g_last[s][:].to_broadcast(tile), mul).then_inc(sdec_ready, 1)

            pool.wait_ge(masks_loaded, 16)
            for m in range(3):
                scale(m, m, m // 2 + 1)
                scale_more(m, m)
                if m < 2:
                    first_inverse(m)
            with pool.Fori(0, NCH) as c:
                with pool.Fori(0, B // TURN) as q:
                    for s in range(TURN):
                        n = c * B + q * TURN + s
                        scale(n + 3, (s + 3) % TURN, c * (B // 2) + q * (TURN // 2) + (s + 3) // 2 + 1)
                        first_inverse(n + 2)
                        decay_state(n, s)
                        scale_more(n + 3, (s + 3) % TURN)

        @block.vector
        def _(dve):
            tr = nc.vector.transpose

            def scans(m, s):
                dve.wait_ge(decays_ready, m + 1)
                dve.wait_ge(kw_ready, m)
                dve.wait_ge(pt_ready, m)
                dve.wait_ge(dpair_ready, m)
                flat = "p g i -> p (g i)"
                nc.vector.tensor_tensor_scan(dmat[:].rearrange(flat), decays[:, 0, :], masks[:, DELTA, :], 0.0,
                                             ALU.mult, ALU.add).then_inc(dmat_ready, 1)
                dve.wait_ge(gqk_ready, m)
                nc.vector.tensor_tensor_scan(gam[:].rearrange(flat), decays[:, 0, :], decays[:, 1, :], 0.0,
                                             ALU.mult, ALU.add).then_inc(gam_ready, 1)
                dve.wait_ge(kb_ready, m + 1)
                tr(kb_t[:], kb[s % 2][:]).then_inc(kbt_ready, 1)

            def triangles(m, s):
                dve.wait_ge(scores_done, m + 1)
                dve.wait_ge(dpair_ready, m + 1)
                dve.wait_ge(a_squared, m)
                dve.wait_ge(g_ready, m)
                dve.wait_ge(t2_ready, m)
                nc.vector.tensor_tensor(a_pair[:], ps_scores[:, :, 1, :].unsqueeze(1).to_broadcast(pair), d_pair[:],
                                        ALU.mult).then_inc(apair_ready, 1)
                dve.wait_ge(apair_ready, m + 1)
                tr(a_in_t[:], a_pair[:, 0]).then_inc(aint_ready, 1)
                dve.wait_ge(kw_ready, m + 1)
                nc.vector.tensor_tensor(kwp[s][:, 1], ps_scores[:, :, 0, :], dmat[:], ALU.mult).then_inc(pt_ready, 1)

            def inverse(n):
                dve.wait_ge(f4_done, n + 1)
                dve.wait_ge(y2_ready, n + 1)
                dve.wait_ge(solved, n)
                nc.vector.tensor_tensor(inv_t[:], y2[:], ps_f4[:, :, 0, :], ALU.add).then_inc(inv_ready, 1)

            def residual(n, s, loads):
                dve.wait_ge(v_loaded[s % 2], 16 * loads)
                dve.wait_ge(read_done, n + 1)
                dve.wait_ge(z_ready, n)
                nc.vector.tensor_tensor(z_t[:], vt[s % 2][:], ps_chain[:, :, 2, :], ALU.subtract).then_inc(zt_ready, 1)
                dve.wait_ge(zt_ready, n + 1)
                dve.wait_ge(solved, n)
                tr(z[:], z_t[:]).then_inc(z_ready, 1)

            def after_a(m):
                dve.wait_ge(a_squared, m + 1)
                dve.wait_ge(tg_done, m)
                tr(a2_t[:], ps_a[:, :, 0, :]).then_inc(a2t_ready, 1)
                dve.wait_ge(tf_ready, m)
                nc.vector.tensor_tensor(tg[:, 1], a_pair[:, 1], ps_a[:, :, 1, :], ALU.subtract).then_inc(g_ready, 1)

            def after_f(m):
                dve.wait_ge(f_squared, m + 1)
                dve.wait_ge(f2_squared, m)
                dve.wait_ge(y2_ready, m)
                nc.vector.tensor_tensor(yf[:, 0], tf[:, 0], ps_f[:, :, 0, :], ALU.subtract).then_inc(y1_ready, 1)
                tr(f2_t[:], ps_f[:, :, 1, :]).then_inc(f2t_ready, 1)

            def after_tg(m):
                dve.wait_ge(tg_done, m + 1)
                dve.wait_ge(t2_ready, m + 1)
                dve.wait_ge(g_ready, m + 1)
                dve.wait_ge(f_squared, m)
                dve.wait_ge(y1_ready, m)
                nc.vector.tensor_tensor(tf[:], tg[:], both(ps_tg), ALU.add).then_inc(tf_ready, 1)
                dve.wait_ge(tf_ready, m + 1)
                tr(f_t[:], tf[:, 1]).then_inc(ft_ready, 1)

            def after_f2(m):
                dve.wait_ge(f2_squared, m + 1)
                dve.wait_ge(f4_done, m)
                tr(f4_t[:], ps_f2[:, :, 1, :]).then_inc(f4t_ready, 1)
                dve.wait_ge(y1_ready, m + 1)
                dve.wait_ge(inv_ready, m)
                nc.vector.tensor_tensor(y2[:], yf[:, 0], ps_f2[:, :, 0, :], ALU.add).then_inc(y2_ready, 1)

            def turn_state(n):
                dve.wait_ge(cur_ready, n + 1)
                dve.wait_ge(read_done, n)
                tr(s_cur_t[:], s_cur[:]).then_inc(curt_ready, 1)

            def new_state(n, b):
                dve.wait_ge(o_ready, n + 1)
                dve.wait_ge(sdec_ready, n + 1)
                nc.vector.tensor_tensor(state[:, bass.ds(b, 1), :, :].rearrange("p a g i -> p (a g) i"), s_decayed[:],
                                        ps_chain[:, :, 0, :], ALU.add).then_inc(state_ready, 1)

            nc.vector.memset(state[:], 0.0).then_inc(state_zero, 1)
            dve.wait_ge(masks_loaded, 16)
            scans(0, 0)
            triangles(0, 0)
            scans(1, 1)
            after_a(0)
            after_tg(0)
            triangles(1, 1)
            after_a(1)
            scans(2, 2)
            after_f(0)
            after_tg(1)
            after_f2(0)
            turn_state(0)
            with dve.Fori(0, NCH) as c:
                with dve.Fori(0, B // TURN) as q:
                    for s in range(TURN):
                        n = c * B + q * TURN + s
                        triangles(n + 2, (s + 2) % TURN)
                        inverse(n)
                        residual(n, s, c * (B // 2) + q * (TURN // 2) + s // 2 + 1)
                        after_a(n + 2)
                        after_f(n + 1)
                        scans(n + 3, (s + 3) % TURN)
                        after_tg(n + 2)
                        after_f2(n + 1)
                        turn_state(n + 1)
                        new_state(n, q * TURN + s)

        @block.scalar
        def _(act):
            def f_square(m):
                act.wait_ge(f2t_ready, m + 1)
                act.wait_ge(f2_squared, m)
                nc.scalar.activation(yf[:, 1], ps_f[:, :, 1, :], ACT.Copy).then_inc(f2_ready, 1)

            def update(n):
                act.wait_ge(solved, n + 1)
                act.wait_ge(wrote, n)
                nc.scalar.activation(u[:], ps_u[:, :, 0, :], ACT.Copy).then_inc(u_ready, 1)

            def output(n, b, c):
                act.wait_ge(wrote, n + 1)
                nc.scalar.activation(o_all[:, bass.ds(b, 1), :, bass.ds(c * CH, CH)].rearrange("p a g i -> p (a g) i"),
                                     ps_chain[:, :, 1, :], ACT.Copy).then_inc(o_ready, 1)

            def current(n, b):
                act.wait_ge(sdec_ready, n)
                act.wait_ge(curt_ready, n)
                nc.scalar.activation(s_cur[:], state[:, bass.ds(b, 1), :, :].rearrange("p a g i -> p (a g) i"),
                                     ACT.Copy).then_inc(cur_ready, 1)

            act.wait_ge(state_zero, 1)
            current(0, 0)
            f_square(0)
            with act.Fori(0, NCH) as c:
                with act.Fori(0, B // TURN) as q:
                    for s in range(TURN):
                        n = c * B + q * TURN + s
                        f_square(n + 1)
                        update(n)
                        act.wait_ge(state_ready, n)
                        if s < TURN - 1:
                            current(n + 1, q * TURN + s + 1)
                        else:
                            current(n + 1, (q + 1) % 2 * TURN)
                        output(n, q * TURN + s, c)

        @block.tensor
        def _(pe):
            def per_head(out, lhs_t, rhs, done, restart=True):
                pe.sem_inc(pe_turns, 1)
                for g in range(KT):
                    for h in range(HG):
                        rows = slice(h * HD, (h + 1) * HD)
                        last = nc.tensor.matmul(out(rows, g), lhs_t(rows, g), rhs(rows, g), start=restart and g == 0,
                                                stop=True, skip_group_check=True)
                last.then_inc(done, 1)

            def scores(m, s):
                pe.wait_ge(kb_ready, m + 1)
                pe.wait_ge(pt_ready, m)
                per_head(lambda r, g: ps_scores[r, g, :, :], lambda r, g: kb[s % 2][r, g, :],
                         lambda r, g: inb[s % 2][r, NQ:NK_ + 1, g, :], scores_done)

            def a_square(m):
                pe.wait_ge(aint_ready, m + 1)
                pe.wait_ge(g_ready, m)
                per_head(lambda r, g: ps_a[r, g, :, :], lambda r, g: a_in_t[r, g, :], lambda r, g: a_pair[r, :, g, :], a_squared)

            def blocks(m):
                pe.wait_ge(a2t_ready, m + 1)
                pe.wait_ge(t2_ready, m + 1)
                pe.wait_ge(g_ready, m + 1)
                pe.wait_ge(tf_ready, m)
                per_head(lambda r, g: ps_tg[r, g, :, :], lambda r, g: a2_t[r, g, :], lambda r, g: tg[r, :, g, :], tg_done)

            def f_square(m):
                pe.wait_ge(ft_ready, m + 1)
                pe.wait_ge(f2_ready, m)
                per_head(lambda r, g: ps_f[r, g, :, :], lambda r, g: f_t[r, g, :], lambda r, g: tf[r, :, g, :], f_squared)

            def f_fourth(m):
                pe.wait_ge(y1_ready, m + 1)
                pe.wait_ge(f2_ready, m + 1)
                pe.wait_ge(y2_ready, m)
                per_head(lambda r, g: ps_f2[r, g, :, :], lambda r, g: f2_t[r, g, :], lambda r, g: yf[r, :, g, :], f2_squared)

            def inverse(n):
                pe.wait_ge(f4t_ready, n + 1)
                pe.wait_ge(y2_ready, n + 1)
                pe.wait_ge(inv_ready, n)
                per_head(lambda r, g: ps_f4[r, g, 0, :], lambda r, g: f4_t[r, g, :], lambda r, g: y2[r, g, :], f4_done)

            def from_state(n, s):
                pe.wait_ge(curt_ready, n + 1)
                pe.wait_ge(gqk_ready, n + 1)
                pe.wait_ge(state_ready, n)
                per_head(lambda r, g: ps_chain[r, g, 1:3, :], lambda r, g: s_cur_t[r, g, :], lambda r, g: gqk[s][r, :, g, :],
                         read_done)

            def solve(n):
                pe.wait_ge(z_ready, n + 1)
                pe.wait_ge(inv_ready, n + 1)
                pe.wait_ge(u_ready, n)
                per_head(lambda r, g: ps_u[r, g, 0, :], lambda r, g: inv_t[r, g, :], lambda r, g: z[r, g, :], solved)

            def into_state(n, s):
                pe.wait_ge(u_ready, n + 1)
                pe.wait_ge(kw_ready, n + 1)
                pe.wait_ge(pt_ready, n + 1)
                per_head(lambda r, g: ps_chain[r, g, 0:2, :], lambda r, g: u[r, g, :], lambda r, g: kwp[s][r, :, g, :], wrote,
                         restart=False)

            scores(0, 0)
            a_square(0)
            blocks(0)
            scores(1, 1)
            a_square(1)
            f_square(0)
            blocks(1)
            f_fourth(0)
            with pe.Fori(0, NCH) as c:
                with pe.Fori(0, B // TURN) as q:
                    for s in range(TURN):
                        n = c * B + q * TURN + s
                        scores(n + 2, s + 2)
                        inverse(n)
                        from_state(n, s)
                        a_square(n + 2)
                        f_square(n + 1)
                        solve(n)
                        blocks(n + 2)
                        f_fourth(n + 1)
                        into_state(n, s)


def attn_out_phase(nc, tag, o_all, gate_dram, src, dst, wo_dram, vec_dram):
    with ExitStack() as ctx:
        def sb(name, shape, dt=F32):
            return ctx.enter_context(nc.sbuf_tensor(f"{tag}_{name}", shape, dt))

        def sem(name):
            return nc.alloc_semaphore(f"{tag}_{name}")

        w_hi, w_lo = sb("w_hi", [P, KT, C], F32R), sb("w_lo", [P, KT, C], F32R)
        gated = [sb(f"gated{s}", [P, KT, TOK]) for s in range(2)]
        high = [sb(f"high{s}", [P, KT, TOK], F32R) for s in range(2)]
        low = [sb(f"low{s}", [P, KT, TOK], F32R) for s in range(2)]
        x = sb("x", [P, KT, TOK])
        vec = sb("vec", [P, 3, KT])
        head_mean = sb("head_mean", [P, P])
        parts = sb("parts", [P, KT, TPB, 6])
        moments = sb("moments", [P, KT, 2])
        head = sb("head", [P, KT, 2])
        m2, var, std, rstd = (sb(n, [P, KT]) for n in ("m2", "var", "std", "rstd"))
        scale, shift, mu_scale = (sb(n, [P, KT]) for n in ("scale", "shift", "mu_scale"))
        ps_head = ctx.enter_context(nc.psum_tensor(f"{tag}_ps_head", [P, TOK], F32))
        ring = [ctx.enter_context(nc.psum_tensor(f"{tag}_ring{n}", [P, TOK], F32)) for n in range(KT)]

        aggregated = sem("aggregated")
        w_loaded, w_split, ready, pool_step = sem("w_loaded"), sem("w_split"), sem("ready"), sem("pool_step")
        gate_loaded = [sem("gate_loaded0"), sem("gate_loaded1")]
        x_loaded, stored = sem("x_loaded"), sem("stored")
        stat_step, head_summed, rooted, scaled = sem("stat_step"), sem("head_summed"), sem("rooted"), sem("scaled")
        normed, gate_used, high_ready, low_ready = sem("normed"), sem("gate_used"), sem("high_ready"), sem("low_ready")
        projected, added = sem("projected"), sem("added")

        block = ctx.enter_context(nc.Block())

        @block.sync
        def _(sp):
            def load_gate(t, s):
                sp.dma_start(gated[s][:], gate_dram[t, :, :, :]).then_inc(gate_loaded[s], 16)

            sp.dma_start(x[:], wo_dram).then_inc(w_loaded, 16)
            sp.dma_start(vec[:], vec_dram).then_inc(w_loaded, 16)
            for s in range(2):
                load_gate(s, s)
            sp.wait_ge(w_split, 2)
            sp.dma_start(x[:], src[0, :, :, :]).then_inc(x_loaded, 16)

            def slot(t, s, next_gate, next_x):
                if next_gate:
                    sp.wait_ge(low_ready, t + 1)
                    load_gate(t + 2, s)
                sp.wait_ge(added, KT * t + KT)
                sp.dma_start(dst[t, :, :, :], x[:]).then_inc(stored, 16)
                if next_x:
                    sp.wait_ge(stored, 16 * t + 16)
                    sp.dma_start(x[:], src[t + 1, :, :, :]).then_inc(x_loaded, 16)

            with sp.Fori(0, B - 1) as b:
                for s in range(TPB):
                    slot(b * TPB + s, s, True, True)
            for s in range(TPB):
                slot(NT - TPB + s, s, False, s + 1 < TPB)
            sp.wait_ge(stored, 16 * NT)

        @block.vector
        def _(dve):
            STEPS = 12
            count = [w_split, 0]
            dve.wait_ge(w_loaded, 32)
            split_weight(nc, dve, x[:], w_hi[:], w_lo[:], count)
            dve.wait_ge(w_split, count[1])
            nc.vector.memset(parts[:], 0.0).then_inc(ready, 1)
            dve.wait_ge(ready, 1)

            def statistics(b):
                at = STEPS * b

                def step(n):
                    dve.wait_ge(stat_step, at + n)

                for g in range(KT):
                    for half in range(TPB):
                        last = nc.vector.bn_stats(parts[:, g, half, :],
                                                  o_all[:, bass.ds(b, 1), g, half * TOK:(half + 1) * TOK].rearrange("p a t -> p (a t)"))
                last.then_inc(stat_step, 1)
                step(1)
                dve.sem_inc(aggregated, 1)
                for g in range(KT):
                    last = nc.vector.bn_aggr(moments[:, g, :], parts[:, g, :, :].rearrange("p a s -> p (a s)"))
                last.then_inc(stat_step, 1)
                step(2)
                nc.vector.tensor_tensor(m2[:], moments[:, :, 0], moments[:, :, 0], ALU.mult).then_inc(stat_step, 1)
                step(3)
                nc.vector.tensor_tensor(moments[:, :, 1], moments[:, :, 1], m2[:], ALU.add).then_inc(stat_step, 1)
                dve.wait_ge(head_summed, b + 1)
                nc.vector.tensor_copy(head[:].rearrange("p g s -> p (g s)"), ps_head[:, 0:2 * KT]).then_inc(stat_step, 1)
                step(5)
                nc.vector.tensor_tensor(m2[:], head[:, :, 0], head[:, :, 0], ALU.mult).then_inc(stat_step, 1)
                step(6)
                nc.vector.tensor_tensor(var[:], head[:, :, 1], m2[:], ALU.subtract).then_inc(stat_step, 1)
                step(7)
                nc.vector.tensor_scalar_add(var[:], var[:], 1e-5).then_inc(stat_step, 1)
                dve.wait_ge(rooted, b + 1)
                nc.vector.reciprocal(rstd[:], std[:]).then_inc(stat_step, 1)
                step(9)
                dve.wait_ge(normed, TPB * b)
                nc.vector.tensor_tensor(scale[:], rstd[:], vec[:, 0, :], ALU.mult).then_inc(stat_step, 1)
                step(10)
                nc.vector.tensor_tensor(mu_scale[:], head[:, :, 0], scale[:], ALU.mult).then_inc(stat_step, 1)
                step(11)
                nc.vector.tensor_tensor(shift[:], vec[:, 1, :], mu_scale[:], ALU.subtract).then_inc(stat_step, 1)
                step(12)
                nc.vector.tensor_copy(mu_scale[:], scale[:]).then_inc(scaled, 1)
                dve.wait_ge(scaled, b + 1)

            def prepare(t, b, s):
                dve.wait_ge(normed, t + 1)
                dve.wait_ge(gate_loaded[s], 16 * b + 16)
                nc.vector.tensor_tensor(gated[s][:], gated[s][:],
                                        o_all[:, bass.ds(b, 1), :, s * TOK:(s + 1) * TOK].rearrange("p a g t -> p (a g) t"),
                                        ALU.mult).then_inc(gate_used, 1)
                dve.wait_ge(high_ready, t + 1)
                nc.vector.tensor_tensor(low[s][:], gated[s][:], high[s][:].bitcast(F32), ALU.subtract).then_inc(low_ready, 1)

            def finish(t):
                dve.wait_ge(x_loaded, 16 * t + 16)
                for m in range(KT):
                    dve.wait_ge(projected, KT * t + m + 1)
                    nc.vector.scalar_tensor_tensor(out=x[:, m, :], in0=ring[m][:], scalar=vec[:, 2, m:m + 1], in1=x[:, m, :],
                                                   op0=ALU.add, op1=ALU.add).then_inc(added, 1)

            def sequence(b, more):
                prepare(b * TPB + 1, b, 1)
                if more:
                    statistics(b + 1)
                finish(b * TPB)
                if more:
                    prepare(b * TPB + 2, b + 1, 0)
                finish(b * TPB + 1)

            statistics(0)
            prepare(0, 0, 0)
            with dve.Fori(0, B - 1) as b:
                sequence(b, True)
            sequence(B - 1, False)

        @block.gpsimd
        def _(pool):
            view = head_mean[:].rearrange("p (h d) -> p h d", h=HG)
            nc.gpsimd.memset(head_mean[:], 1.0 / HD).then_inc(pool_step, 1)
            pool.wait_ge(pool_step, 1)
            nc.gpsimd.affine_select(out=view, in_=view, compare_op=ALU.is_ge, fill=0.0, base=0,
                                    pattern=[[-HD, HG], [0, HD]], channel_multiplier=1).then_inc(pool_step, 1)
            pool.wait_ge(pool_step, 2)
            nc.gpsimd.affine_select(out=view, in_=view, compare_op=ALU.is_ge, fill=0.0, base=HD - 1,
                                    pattern=[[HD, HG], [0, HD]], channel_multiplier=-1).then_inc(pool_step, 1)

        @block.scalar
        def _(act):
            def root(b):
                act.wait_ge(stat_step, 12 * b + 8)
                nc.scalar.activation(std[:], var[:], ACT.Sqrt).then_inc(rooted, 1)

            def norm(t, b, s):
                act.wait_ge(scaled, b + 1)
                for g in range(KT):
                    view = o_all[:, bass.ds(b, 1), g, s * TOK:(s + 1) * TOK].rearrange("p a t -> p (a t)")
                    last = nc.scalar.activation(view, view, ACT.Identity, bias=shift[:, g:g + 1], scale=scale[:, g:g + 1])
                last.then_inc(normed, 1)
                act.wait_ge(gate_used, t + 1)
                nc.scalar.activation(high[s][:], gated[s][:], ACT.Copy).then_inc(high_ready, 1)

            def sequence(b, more):
                act.wait_ge(projected, KT * TPB * b)
                norm(b * TPB + 1, b, 1)
                if more:
                    root(b + 1)
                    act.wait_ge(projected, KT * TPB * b + KT)
                    norm(b * TPB + 2, b + 1, 0)

            act.wait_ge(ready, 1)
            root(0)
            norm(0, 0, 0)
            with act.Fori(0, B - 1) as b:
                sequence(b, True)
            sequence(B - 1, False)

        @block.tensor
        def _(pe):
            def head_stats(b):
                pe.wait_ge(stat_step, 12 * b + 4)
                nc.tensor.matmul(ps_head[:, 0:2 * KT], head_mean[:], moments[:].rearrange("p g s -> p (g s)"),
                                 start=True, stop=True).then_inc(head_summed, 1)

            def project(t, s):
                pe.wait_ge(low_ready, t + 1)
                pe.wait_ge(added, KT * t)
                for m in range(KT):
                    product(nc, ring[m][:], w_hi, w_lo, m, high[s], low[s]).then_inc(projected, 1)

            def sequence(b, more):
                project(b * TPB, 0)
                if more:
                    head_stats(b + 1)
                project(b * TPB + 1, 1)

            pe.wait_ge(pool_step, 3)
            pe.wait_ge(ready, 1)
            head_stats(0)
            with pe.Fori(0, B - 1) as b:
                sequence(b, True)
            sequence(B - 1, False)


def macaron_block(nc, x, masks, ffn_w, ffn_mu, attn_w, wab, attn_bias, ab_bias, taps, wo, out_vec, out):
    x1 = nc.dram_tensor("x1", [NT, P, KT, TOK], F32).ap()
    x2 = nc.dram_tensor("x2", [NT, P, KT, TOK], F32).ap()
    gate = nc.dram_tensor("gate", [NT, P, KT, TOK], F32).ap()
    streams = nc.dram_tensor("streams", [B * NCH, P, 5 * KT * CH], F32).ap()
    with nc.cleanup_on_exit():
        ffn_phase(nc, "ffn1", x, x1, ffn_w, ffn_mu)
    with nc.cleanup_on_exit():
        attn_in_phase(nc, "ain", x1, streams, gate, attn_w, wab, attn_bias, ab_bias, taps)
    with nc.sbuf_tensor("o_all", [P, B, KT, S], F32) as o_all:
        with nc.cleanup_on_exit():
            recurrence_phase(nc, "rec", streams, masks, o_all)
        with nc.cleanup_on_exit():
            attn_out_phase(nc, "aout", o_all, gate, x1, x2, wo, out_vec)
    with nc.cleanup_on_exit():
        ffn_phase(nc, "ffn2", x2, out, ffn_w, ffn_mu)



def kernel(**inputs):
    import numpy as np
    import concourse.bacc as bacc
    from concourse.bass_utils import run_bass_kernel_spmd

    a = {name: np.asarray(value) for name, value in inputs.items()}
    attn = {name[len("L0_attn_"):]: value for name, value in a.items() if name.startswith("L0_attn_")}
    ffn = {name[len("L0_ffn_"):]: value for name, value in a.items() if name.startswith("L0_ffn_")}

    def tiles(x):
        return np.ascontiguousarray(x.reshape(NT, TOK, KT, P).transpose(0, 3, 2, 1))

    def weight(w):
        return np.ascontiguousarray(w.reshape(KT, P, -1).transpose(1, 0, 2))

    def vectors(vs):
        return np.ascontiguousarray(np.stack(vs).reshape(len(vs), KT, P).transpose(2, 0, 1))

    arrays = {
        "in_x": tiles(attn["x"].reshape(B * S, C)),
        "in_masks": recurrence_masks(),
        **{f"in_ffn_{n}": weight(ffn[f"W_{n}"].T) for n in "rkv"},
        "in_mu": vectors([ffn["mu_r"], ffn["mu_k"]]),
        **{f"in_w{n}": weight(attn[f"W{n}"]) for n in "qkvg"},
        "in_wab": weight(np.concatenate([attn["Wa"], attn["Wb"]], axis=1)),
        "in_bias": vectors([attn[f"b{n}"] for n in "qkvg"]),
        "in_ab_bias": np.ascontiguousarray(np.concatenate([attn["ba"], attn["bb"]])[:, None]),
        "in_taps": np.ascontiguousarray(np.stack([attn[f"{n}_conv"] for n in "qkv"])
                                        .reshape(3, KT, P, TAPS).transpose(2, 0, 1, 3)),
        "in_wo": weight(attn["Wo"]),
        "in_out_vec": vectors([attn["gn_scale"], attn["gn_bias"], attn["bo"]]),
    }
    nc = bacc.Bacc("TRN2", target_bir_lowering=False, num_devices=1)
    d = {name: nc.dram_tensor(name, v.shape, mybir.dt.from_np(v.dtype), kind="ExternalInput").ap() for name, v in arrays.items()}
    out = nc.dram_tensor("out", [NT, P, KT, TOK], F32, kind="ExternalOutput").ap()
    macaron_block(nc, d["in_x"], d["in_masks"], {n: d[f"in_ffn_{n}"] for n in "rkv"}, d["in_mu"],
                  {n: d[f"in_w{n}"] for n in "qkvg"}, d["in_wab"], d["in_bias"], d["in_ab_bias"], d["in_taps"],
                  d["in_wo"], d["in_out_vec"], out)
    r = run_bass_kernel_spmd(nc, [arrays], core_ids=[0])
    got = r.results[0]["out"]
    return np.ascontiguousarray(got.transpose(0, 3, 2, 1)).reshape(B, S, C)
```
